# Optimizing a Trainium2 kernel written in Bass

```python
import numpy as np
import jax
import jax.numpy as jnp

def _softmax(x, axis=-1):
    return jax.nn.softmax(x, axis=axis)
def _gelu(x):
    return jax.nn.gelu(x, approximate=True)
def _silu(x):
    return jax.nn.silu(x)
def _sigmoid(x):
    return jax.nn.sigmoid(x)
def _layernorm(x, axis=-1, eps=1e-5):
    m = jnp.mean(x, axis=axis, keepdims=True)
    v = jnp.var(x, axis=axis, keepdims=True)
    return (x - m) / jnp.sqrt(v + eps)
def _scatter_add(tgt, idx, src, axis=0):
    return tgt.at[idx].add(src)
def _segment_sum(src, seg, n):
    return jax.ops.segment_sum(src, seg, n)

kernel_name = 'mk_adj_preln_d1_adj_512_7e2f4b'

def setup_inputs(seed: int = 0):
    np.random.seed(seed)
    _w = jnp.asarray
    def _rec_inputs():
        import jax
        import jax.numpy as jnp
        _gk = jax.random.key(seed)
        x = -0.0005963 + 1.001 * jax.random.normal(jax.random.fold_in(_gk, 1), (6144, 512), jnp.float32)
        _a = jax.random.bernoulli(jax.random.fold_in(_gk, 2), 0.00260417, (6144, 6144))
        _a = jnp.logical_or(_a, jnp.swapaxes(_a, -1, -2))
        _a = jnp.logical_or(_a, jnp.eye(6144, dtype=bool))
        adj = _a.astype(jnp.int32)
        return x, adj
    x, adj = _rec_inputs()
    def _L0_gnn_setup():
        import jax, jax.numpy as jnp
        import numpy as np
        N = 6144
        IN_F = 512
        H = 8
        DH = 64
        ALPHA = 0.2
        NEG = -1000000000.0
        key = jax.random.key(seed)
        k1, k2, k3, k4, k5 = jax.random.split(key, 5)
        x = jax.random.normal(k1, (N, IN_F), dtype=jnp.float32)
        adj = jax.random.randint(k2, (N, N), 0, 2, dtype=jnp.int32)
        W = jax.random.normal(k3, (H * DH, IN_F), dtype=jnp.float32) * (2.0 / (IN_F + H * DH)) ** 0.5
        b = jnp.zeros((H * DH,), dtype=jnp.float32)
        aw = jax.random.normal(k4, (H, DH, 2), dtype=jnp.float32) * (2.0 / (DH + 2)) ** 0.5
        return {'x': x, 'adj': adj, 'W': W, 'b': b, 'aw': aw}
    _L0_gnn_all = _L0_gnn_setup()
    _L0_gnn_in = {k: v for k, v in _L0_gnn_all.items() if k in ('W', 'b', 'aw', )}
    del _L0_gnn_all

    return {
        "x": x,
        "adj": adj,
        "L0_gnn_W": _L0_gnn_in["W"],
        "L0_gnn_b": _L0_gnn_in["b"],
        "L0_gnn_aw": _L0_gnn_in["aw"],
    }

def reference(x, adj, L0_gnn_W, L0_gnn_b, L0_gnn_aw):
    import jax
    import jax.numpy as jnp
    def _L0_gnn_ref(x, adj, W, b, aw):
        import jax, jax.numpy as jnp
        import numpy as np
        N = 6144
        IN_F = 512
        H = 8
        DH = 64
        ALPHA = 0.2
        NEG = -1000000000.0
        h = (x @ W.T + b).reshape(N, H, DH).transpose(1, 0, 2)
        a = jnp.einsum('hnd,hdk->hnk', h, aw)
        scores = jax.nn.leaky_relu(a[:, :, 0][:, :, None] + a[:, :, 1][:, None, :], ALPHA)
        mask = (adj > 0)[None, :, :]
        scores = jnp.where(mask, scores, NEG)
        p = jax.nn.softmax(scores, axis=2)
        p = jnp.where(mask, p, 0.0)
        out = jnp.einsum('hij,hjd->hid', p, h)
        out = out.transpose(1, 0, 2).reshape(N, H * DH)
        return out

    h = jnp.maximum(_layernorm(x, axis=-1), 0.0)
    x = x + _L0_gnn_ref(h, adj, L0_gnn_W, L0_gnn_b, L0_gnn_aw)
    return x


_drawn_inputs = setup_inputs


def setup_inputs(seed=0):
    import zlib

    import numpy as np

    out = dict(_drawn_inputs(seed))
    spreads = {'L0_gnn_b': (0.0, 0.1)}
    factors = {}
    for name, (base, spread) in spreads.items():
        noise = np.random.default_rng([zlib.crc32(name.encode()), seed]).standard_normal(out[name].shape)
        drawn = base * np.exp(spread * noise) if base else spread * noise
        out[name] = jnp.asarray(drawn.astype(out[name].dtype))
    for name, factor in factors.items():
        out[name] = (out[name] * factor).astype(out[name].dtype)
    return out
```

```python
import concourse.bass as bass
from concourse import mybir
from contextlib import ExitStack

F32 = mybir.dt.float32
BF16 = mybir.dt.bfloat16
FP8 = mybir.dt.float8e4
I32 = mybir.dt.int32
I8 = mybir.dt.int8
U8 = mybir.dt.uint8
ALU = mybir.AluOpType
ACT = mybir.ActivationFunctionType
AX = mybir.AxisListType


P = 128
N = 6144
F = 512
H = 8
DH = 64
ALPHA = 0.2
EPS = 1e-5
NT = N // P
BITS = (0x40, 0x20, 0x10, 0x08)
BIT_INVERSE = (0.5, 8.0, 32.0, 64.0)
NB = len(BITS)
NQ = NT // NB
IB = 512
IT = IB // P
NIB = N // IB
GK = 4
NG = NT // GK
NQG = NQ // GK
W1 = DH + 1
PARTS = 3
MW = PARTS * W1
KC = F // P
SLOTS = 3
HEADROOM = 86
SIGNS = 3


class Count:

    def __init__(self, eng, name, first, by=1):
        self.eng = eng
        self.by = by
        self.reg = eng.alloc_register(name)
        eng.reg_mov(self.reg, first)

    def wait(self, sem):
        self.eng.wait_ge(sem, self.reg)
        self.eng.reg_add(self.reg, self.reg, self.by)


def gat_kernel(nc, x, adj, w, b, aw, h_dram, s_dram, out):
    ctx = ExitStack()
    with ctx:
        def sb(name, shape, dt):
            return ctx.enter_context(nc.sbuf_tensor(name, shape, dt))

        def ps(name, shape, dt):
            return ctx.enter_context(nc.psum_tensor(name, shape, dt))

        def sem(name):
            return ctx.enter_context(nc.semaphore(name))

        packed = sb("packed", [P, NQ, N], U8)
        t_sb = sb("t_sb", [P, H, NT], F32)
        neg_t = sb("neg_t", [P, H, NT], F32)
        coef = sb("coef", [P, IT + H * NT, 2], F32)
        wxy = sb("wxy", [P, H * NT, 2], F32)
        big = sb("big", [P, 2 * NT * 2 * MW], BF16)
        xy = big[:, :].rearrange("p (a t c m) -> p a t c m", a=2, t=NT, c=2)
        adj_raw = big[:, 0:4 * N].bitcast(I32).rearrange("p (a n) -> p a n", a=2)
        adj01 = big[:, 4 * N:6 * N].rearrange("p (a n) -> p a n", a=2)

        ARENA = 48 * 256
        arena = sb("arena", [P, ARENA], F32)

        def layout():
            at = [0]

            def carve(words, parts=P):
                at[0] += words
                assert at[0] <= ARENA, at[0]
                return arena[0:parts, at[0] - words:at[0]]
            return carve

        carve = layout()
        w_nat = carve(KC * F).rearrange("p (c f) -> p c f", c=KC)
        wt = carve(KC * F).rearrange("p (k n) -> p k n", k=KC)
        x_in = carve(2 * F).rearrange("p (a f) -> p a f", a=2)
        xn = carve(2 * F).rearrange("p (a f) -> p a f", a=2)
        hn_t = carve(2 * F).rearrange("p (a k i) -> p a k i", a=2, k=KC)
        h_sb = carve(2 * F).rearrange("p (a f) -> p a f", a=2)
        b_bc = carve(F)
        b_rep = carve(KC * P).rearrange("p (c m) -> p c m", c=KC)
        ident = carve(P)
        ident_bits = carve(NB * P // 2).bitcast(BF16).rearrange("p (b m) -> p b m", b=NB)
        wa = carve(KC * 2 * H).rearrange("p (k m) -> p k m", k=KC)
        ba = carve(2 * H)
        aw_blk = carve(KC * 2 * H).rearrange("p (c m) -> p c m", c=KC)
        b_col = carve(KC)
        st_cols = carve(2 * H * (NT + 1)).rearrange("p (m t) -> p m t", t=NT + 1)
        st_all = st_cols[:, :, 1:NT + 1]
        stats = carve(2 * 6).rearrange("p (a m) -> p a m", a=2)
        mv = carve(2 * 2).rearrange("p (a m) -> p a m", a=2)
        ve = carve(2)
        std = carve(2)
        r0 = carve(2)
        r1 = carve(2)
        rstd = carve(2)
        t_max = carve(H)
        t_top = carve(H)
        tmp = [w_nat[:, c, 0:H * NT] for c in range(KC)]
        s_t = wt[0:NT, :, :].rearrange("r k n -> r (k n)")[:, 0:H * P].rearrange("r (h i) -> r h i", h=H)

        carve = layout()
        sgn = carve(SLOTS * GK * IB // 4).bitcast(I8).rearrange("p (s k i) -> p s k i", s=SLOTS, k=GK)
        mask_b = carve(SLOTS * GK * IB // 4).bitcast(I8).rearrange("p (s k i) -> p s k i", s=SLOTS, k=GK)
        mask_c = carve(SLOTS * GK * IB // 4).bitcast(I8).rearrange("p (s k i) -> p s k i", s=SLOTS, k=GK)
        s_bc = carve(2 * IB).rearrange("p (a i) -> p a i", a=2)
        hx = carve(2 * GK * W1).rearrange("p (a k m) -> p a k m", a=2, k=GK)
        prod = carve(GK * 2 * W1).rearrange("p (k c m) -> p k c m", k=GK, c=2)
        rest = carve(GK * 2 * W1).rearrange("p (k c m) -> p k c m", k=GK, c=2)
        low_parts = carve(IT * 2 * (MW - W1)).rearrange("p (t c m) -> p t c m", t=IT, c=2)
        total = carve(IT * 2 * W1).rearrange("p (t c m) -> p t c m", t=IT, c=2)
        scaled = carve(IT * 2 * W1).rearrange("p (t c m) -> p t c m", t=IT, c=2)
        both = carve(IT * W1).rearrange("p (t m) -> p t m", t=IT)
        rden = carve(IT)
        x_res = carve(2 * IT * DH).rearrange("p (a t d) -> p a t d", a=2, t=IT)
        o_sb = carve(2 * IT * DH).rearrange("p (a t d) -> p a t d", a=2, t=IT)

        psum = ps("psum", [P, 8, 512], F32)

        x_rows = x.rearrange("(t p) f -> t p f", p=P)
        adj_rows = adj.rearrange("(t p) j -> t p j", p=P)
        h_rows = h_dram.rearrange("(t p) f -> t p f", p=P)
        h_group = h_dram.rearrange("(g k b p) (h d) -> g b h p k d", p=P, b=NB, k=GK, d=DH)
        x_blk = x.rearrange("(n t p) (h d) -> n h p t d", p=P, t=IT, d=DH)
        out_blk = out.rearrange("(n t p) (h d) -> n h p t d", p=P, t=IT, d=DH)
        s_blk = s_dram.rearrange("h (n i) -> h n i", i=IB)

        w_in = sem("w_in")
        aw_in = sem("aw_in")
        x_loaded = [sem(f"x_loaded{a}") for a in range(2)]
        adj_loaded = [sem(f"adj_loaded{a}") for a in range(2)]
        ident_ready = sem("ident_ready")
        aw_zero = sem("aw_zero")
        brep_ready = sem("brep_ready")
        wt_ps = sem("wt_ps")
        wt_copied = sem("wt_copied")
        wa_ps = sem("wa_ps")
        wa_copied = sem("wa_copied")
        ve_ready = sem("ve_ready")
        std_ready = sem("std_ready")
        xn_ready = sem("xn_ready")
        adj01_ready = sem("adj01_ready")
        pack_done = sem("pack_done")
        pack_copied = sem("pack_copied")
        xt_done = sem("xt_done")
        hnt_ready = sem("hnt_ready")
        h_done = sem("h_done")
        h_ready = sem("h_ready")
        h_stored = [sem(f"h_stored{a}") for a in range(2)]
        chain1 = sem("chain1")
        tmax_ready = sem("tmax_ready")
        top_ready = sem("top_ready")
        arg_ready = sem("arg_ready")
        exp_ready = sem("exp_ready")
        st_ready = sem("st_ready")
        s_ps = sem("s_ps")
        s_copied = sem("s_copied")
        s_stored = sem("s_stored")
        wxy_ready = sem("wxy_ready")
        START = {"xn": 2, "adj01": 2, "pack": 2, "xt": 2, "hnt": 1, "h_done": 2, "h_ready": 1,
                 "pack_copied": 1}

        with nc.Block() as block:

            @block.sync
            def _(sp):
                sp.dma_start(w_nat, w.rearrange("(c p) f -> p c f", p=P)).then_inc(w_in, 16)
                sp.dma_start(b_bc, b.partition_broadcast(P)).then_inc(w_in, 16)
                sp.dma_start(b_col, b.rearrange("(c p) -> p c", p=P), allow_slow_non_contiguous=True).then_inc(w_in, 16)
                with sp.Fori(0, NT // 2) as i:
                    for a in range(2):
                        n = 2 * i + a
                        sp.wait_ge(xn_ready, n + 1)
                        sp.dma_start(x_in[:, a, :], x_rows[n]).then_inc(x_loaded[a], 16)
                        sp.wait_ge(adj01_ready, n + 1)
                        sp.dma_start(adj_raw[:, a, :], adj_rows[n]).then_inc(adj_loaded[a], 16)
                sp.wait_ge(s_copied, 1)
                sp.dma_start(s_dram.rearrange("h (r i) -> r h i", i=P), s_t).then_inc(s_stored, 16)
                sp.wait_ge(s_stored, 16)

            @block.gpsimd
            def _(pool):
                for s, count in ((xn_ready, START["xn"]), (adj01_ready, START["adj01"]),
                                 (pack_done, START["pack"]), (xt_done, START["xt"]),
                                 (hnt_ready, START["hnt"]), (h_done, START["h_done"]),
                                 (h_ready, START["h_ready"]), (pack_copied, START["pack_copied"])):
                    pool.nop().then_inc(s, count)
                pool.memset(aw_blk, 0.0).then_inc(aw_zero, 1)
                pool.memset(ident, 0.0).then_inc(aw_zero, 1)
                pool.wait_ge(aw_zero, 2)
                pool.affine_select(out=ident, in_=ident, compare_op=ALU.not_equal, fill=1.0, base=0,
                                   pattern=[[-1, P]], channel_multiplier=1).then_inc(ident_ready, 1)
                for h in range(H):
                    lo = (h % 2) * DH
                    pool.dma_start(aw_blk[lo:lo + DH, h // 2, h:h + H + 1:H], aw[h], allow_slow_non_contiguous=True).then_inc(aw_in, 16)
                with pool.Fori(0, NT // 2) as i:
                    for a in range(2):
                        n = 2 * i + a
                        pool.wait_ge(h_ready, n + 1 + START["h_ready"])
                        pool.dma_start(h_rows[n], h_sb[:, a, :]).then_inc(h_stored[a], 16)
                pool.wait_ge(tmax_ready, 1)
                pool.partition_all_reduce(t_top, t_max, P, bass.bass_isa.ReduceOp.max).then_inc(top_ready, 1)
                for a in range(2):
                    pool.wait_ge(h_stored[a], 16 * (NT // 2))

            @block.tensor
            def _(pe):
                ps_t = psum[:, 3, :].rearrange("p (k i) -> p k i", k=KC)
                ps_h = psum[:, 4, :]
                ps_st = psum[:, 5, 0:2 * H]
                ps_ba = psum[:, 6, 0:2 * H]
                pe.wait_ge(w_in, 48)
                pe.wait_ge(ident_ready, 1)
                for k in range(KC):
                    if k:
                        pe.wait_ge(wt_copied, k)
                    for c in range(KC):
                        last = nc.tensor.transpose(ps_t[:, c, :], w_nat[:, c, k * P:(k + 1) * P], ident)
                    last.then_inc(wt_ps, 1)
                pe.wait_ge(aw_in, 16 * H)
                pe.wait_ge(brep_ready, 1)
                for k in range(KC):
                    if k:
                        pe.wait_ge(wa_copied, k)
                    for c in range(KC):
                        last = nc.tensor.matmul(ps_st, w_nat[:, c, k * P:(k + 1) * P], aw_blk[:, c, :],
                                                start=(c == 0), stop=(c == KC - 1))
                    last.then_inc(wa_ps, 1)
                for c in range(KC):
                    last = nc.tensor.matmul(ps_ba, b_rep[:, c, :], aw_blk[:, c, :],
                                            start=(c == 0), stop=(c == KC - 1))
                last.then_inc(wa_ps, 1)
                pe.wait_ge(wa_copied, KC + 1)
                pe.wait_ge(wt_copied, KC)

                def pack(a, q):
                    bank, at = q // 4, (q % 4) * P
                    for bit in range(NB):
                        jt = NB * q + bit
                        last = nc.tensor.matmul(psum[:, bank, at:at + P],
                                                adj01[:, a, jt * P:(jt + 1) * P], ident_bits[:, bit, :],
                                                start=(bit == 0), stop=(bit == NB - 1))
                    return last

                with pe.Fori(0, NT // 2) as i:
                    for a in range(2):
                        n = 2 * i + a
                        pe.wait_ge(adj01_ready, n + 1 + START["adj01"])
                        pe.wait_ge(pack_copied, n + START["pack_copied"])
                        for q in range(NQ // 2):
                            pack(a, q)
                        pe.wait_ge(xn_ready, n + 1 + START["xn"])
                        pe.wait_ge(hnt_ready, n + START["hnt"])
                        for k in range(KC):
                            last = nc.tensor.transpose(ps_t[:, k, :], xn[:, a, k * P:(k + 1) * P], ident)
                        last.then_inc(xt_done, 1)
                        for q in range(NQ // 2, NQ):
                            last = pack(a, q)
                        last.then_inc(pack_done, 1)
                        pe.wait_ge(hnt_ready, n + 1 + START["hnt"])
                        pe.wait_ge(h_ready, n + START["h_ready"])
                        for k in range(KC):
                            nc.tensor.matmul(ps_h, hn_t[:, a, k, :], wt[:, k, :],
                                             start=(k == 0), stop=(k == KC - 1))
                        for k in range(KC):
                            last = nc.tensor.matmul(ps_st, hn_t[:, a, k, :], wa[:, k, :],
                                                    start=(k == 0), stop=(k == KC - 1))
                        last.then_inc(h_done, 1)
                pe.wait_ge(st_ready, 1)
                for h in range(H):
                    last = nc.tensor.transpose(psum[0:NT, 6 + h // 4, (h % 4) * P:(h % 4 + 1) * P],
                                               st_all[:, h, :], ident)
                last.then_inc(s_ps, 1)

            @block.scalar
            def _(act):
                for k in range(KC):
                    act.wait_ge(wt_ps, k + 1)
                    act.activation(wt[:, k, :], psum[:, 3, :], ACT.Copy).then_inc(wt_copied, 1)
                with act.Fori(0, NT // 2) as i:
                    for a in range(2):
                        n = 2 * i + a
                        act.wait_ge(ve_ready, n + 1)
                        act.activation(std[:, a:a + 1], ve[:, a:a + 1], ACT.Sqrt).then_inc(std_ready, 1)
                        act.wait_ge(h_done, n + START["h_done"] - 1)
                        act.wait_ge(xt_done, n + 1 + START["xt"])
                        act.activation(hn_t[:, a, :, :], psum[:, 3, :].rearrange("p (k i) -> p k i", k=KC),
                                       ACT.Relu).then_inc(hnt_ready, 1)
                        act.wait_ge(pack_done, n + 1 + START["pack"])
                        act.activation(packed[:, :, bass.ts(n, P)],
                                       psum[:, 0:3, :].rearrange("p k (q i) -> p (k q) i", q=4),
                                       ACT.Copy).then_inc(pack_copied, 1)
                t_less_top = wt[:, 2, 0:H * NT]
                for k, (arg, by) in enumerate(((tmp[0], 1.0), (tmp[1], 0.5), (t_less_top, 0.5),
                                               (t_less_top, ALPHA))):
                    act.wait_ge(arg_ready, min(k + 1, 3))
                    act.activation(tmp[k], arg, ACT.Exp, scale=by).then_inc(exp_ready, 1)

            @block.vector
            def _(dve):
                linked = Count(dve, "linked1", 1)
                h_free = [Count(dve, f"h_free{a}", 16, 16) for a in range(2)]

                def link(ins):
                    ins.then_inc(chain1, 1)
                    linked.wait(chain1)

                dve.wait_ge(w_in, 48)
                dve.tensor_copy(b_rep, b_col.unsqueeze(2).broadcast_to([P, KC, P])).then_inc(brep_ready, 1)
                dve.wait_ge(ident_ready, 1)
                for bit in range(NB):
                    link(dve.tensor_scalar(ident_bits[:, bit, :], ident, float(BITS[bit]), None, ALU.mult))
                for k in range(KC):
                    dve.wait_ge(wa_ps, k + 1)
                    dve.tensor_copy(wa[:, k, :], psum[:, 5, 0:2 * H]).then_inc(wa_copied, 1)
                dve.wait_ge(wa_ps, KC + 1)
                dve.tensor_copy(ba, psum[:, 6, 0:2 * H]).then_inc(wa_copied, 1)
                dve.wait_ge(wa_copied, KC + 1)

                def rows(n, a, half):
                    dve.wait_ge(x_loaded[a], 16 * (half + 1))
                    link(dve.bn_stats(stats[:, a, :], x_in[:, a, :]))
                    link(dve.bn_aggr(mv[:, a, :], stats[:, a, :]))
                    dve.tensor_scalar(ve[:, a:a + 1], mv[:, a, 1:2], EPS, None, ALU.add).then_inc(ve_ready, 1)
                    dve.wait_ge(adj_loaded[a], 16 * (half + 1))
                    dve.wait_ge(pack_done, n + START["pack"] - 1)
                    dve.tensor_scalar(adj01[:, a, :], adj_raw[:, a, :], 0.0, None, ALU.is_gt)\
                       .then_inc(adj01_ready, 1)
                    dve.wait_ge(std_ready, n + 1)
                    link(dve.reciprocal(r0[:, a:a + 1], std[:, a:a + 1]))
                    link(dve.scalar_tensor_tensor(r1[:, a:a + 1], r0[:, a:a + 1], ve[:, a:a + 1],
                                                  r0[:, a:a + 1], ALU.mult, ALU.mult))
                    link(dve.tensor_scalar(r1[:, a:a + 1], r1[:, a:a + 1], -0.5, 1.5, ALU.mult, ALU.add))
                    link(dve.tensor_tensor(rstd[:, a:a + 1], r0[:, a:a + 1], r1[:, a:a + 1], ALU.mult))
                    dve.wait_ge(xt_done, n + START["xt"] - 1)
                    dve.tensor_scalar(xn[:, a, :], x_in[:, a, :], mv[:, a, 0:1], rstd[:, a:a + 1],
                                      ALU.subtract, ALU.mult).then_inc(xn_ready, 1)

                def finish(m_plus_1, a, reused):
                    if reused is True:
                        h_free[a].wait(h_stored[a])
                    else:
                        with dve.If(reused):
                            h_free[a].wait(h_stored[a])
                    dve.wait_ge(h_done, m_plus_1 + START["h_done"])
                    link(dve.tensor_tensor(h_sb[:, a, :], psum[:, 4, :], b_bc, ALU.add))
                    dve.tensor_tensor(st_cols[:, :, bass.ds(m_plus_1, 1)], psum[:, 5, 0:2 * H].unsqueeze(2),
                                      ba.unsqueeze(2), ALU.add).then_inc(h_ready, 1)

                with dve.Fori(0, NT // 2) as i:
                    for a in range(2):
                        n = 2 * i + a
                        rows(n, a, i)
                        if a == 0:
                            with dve.If(i > 0):
                                finish(n, 1, i > 1)
                        else:
                            finish(n, 0, i > 0)
                finish(NT, 1, True)

                dve.wait_ge(h_ready, NT + START["h_ready"])
                dve.nop().then_inc(st_ready, 1)
                s_all = st_all[:, 0:H, :]
                t_all = st_all[:, H:2 * H, :]
                dve.tensor_reduce(t_max, t_all, AX.X, ALU.max).then_inc(tmax_ready, 1)
                link(dve.tensor_copy(t_sb[:, :, :], t_all))
                link(dve.tensor_scalar(neg_t[:, :, :], t_all, -1.0, None, ALU.mult))
                dve.wait_ge(top_ready, 1)
                top = t_top.unsqueeze(2).broadcast_to([P, H, NT])
                v = [t.rearrange("p (h t) -> p h t", h=H) for t in tmp]
                z, guard = (wt[:, c, 0:H * NT].rearrange("p (h t) -> p h t", h=H) for c in range(2, 4))
                link(dve.tensor_tensor(z, s_all, top, ALU.add))
                link(dve.scalar_tensor_tensor(guard, z, ALPHA, z, ALU.mult, ALU.max))
                dve.tensor_tensor(v[0], z, guard, ALU.subtract).then_inc(arg_ready, 1)
                dve.wait_ge(arg_ready, 1)
                dve.scalar_tensor_tensor(v[1], z, ALPHA, guard, ALU.mult, ALU.subtract).then_inc(arg_ready, 1)
                dve.wait_ge(arg_ready, 2)
                dve.tensor_tensor(z, t_all, top, ALU.subtract).then_inc(arg_ready, 1)
                dve.wait_ge(s_ps, 1)
                dve.tensor_copy(s_t, psum[0:NT, 6:8, :].rearrange("r k (h i) -> r (k h) i", h=4))\
                   .then_inc(s_copied, 1)
                dve.wait_ge(s_copied, 1)
                coef_v = coef[:, IT:IT + H * NT, :].rearrange("p (h t) c -> p h t c", h=H)
                wxy_v = wxy[:, :, :].rearrange("p (h g b k) c -> p h g b k c", h=H, g=NQG, b=NB)
                half_room = float(2.0 ** (HEADROOM // 2))
                dve.wait_ge(exp_ready, 1)
                link(dve.tensor_copy(coef_v[:, :, :, 0], v[0]))
                dve.wait_ge(exp_ready, 2)
                link(dve.tensor_scalar(v[1], v[1], half_room, None, ALU.mult))
                link(dve.tensor_tensor(coef_v[:, :, :, 1], v[1], v[1], ALU.mult))
                dve.wait_ge(exp_ready, 3)
                link(dve.tensor_scalar(v[2], v[2], half_room, None, ALU.mult))
                link(dve.tensor_tensor(v[2], v[2], v[2], ALU.mult))
                dve.wait_ge(exp_ready, 4)
                for c in range(2):
                    in_order = v[2 + c].rearrange("p h (g k b) -> p h g b k", g=NQG, b=NB)
                    for bit in range(NB):
                        for g in range(NQG):
                            dve.tensor_scalar(wxy_v[:, :, g, bit, :, c], in_order[:, :, g, bit, :],
                                              BIT_INVERSE[bit], None, ALU.mult).then_inc(wxy_ready, 1)
                dve.wait_ge(wxy_ready, 2 * NB * NQG)

        s_loaded = [sem(f"s_loaded{a}") for a in range(2)]
        xr_loaded = [sem(f"xr_loaded{a}") for a in range(2)]
        hx_loaded = [sem(f"hx_loaded{a}") for a in range(2)]
        hx_ones = sem("hx_ones")
        signs = sem("signs")
        c_ready = sem("c_ready")
        b_ready = sem("b_ready")
        groups_done = sem("groups_done")
        xy_ready = sem("xy_ready")
        acc_free = sem("acc_free")
        low_copied = sem("low_copied")
        result_ready = sem("result_ready")
        out_stored = [sem(f"out_stored{a}") for a in range(2)]
        chain2 = sem("chain2")
        pool_chain = sem("pool_chain")
        STEPS = H * NIB

        def acc(a, t):
            return psum[:, IT * a + t, 0:2 * MW].rearrange("p (c m) -> p c m", c=2)

        def accs(a):
            return psum[:, IT * a:IT * a + IT, 0:2 * MW].rearrange("p t (c m) -> p t c m", c=2)

        def parts(eng, link, at, head, g, a):
            wgt = wxy[:, bass.ds(head * NT + GK * g, GK), :].unsqueeze(3).broadcast_to([P, GK, 2, W1])
            hxb = hx[:, a, :, :].unsqueeze(2).broadcast_to([P, GK, 2, W1])
            dst = xy[:, at, GK * g:GK * g + GK, :, :] if isinstance(g, int) else \
                xy[:, at, bass.ds(GK * g, GK), :, :]
            link(eng.tensor_tensor(prod, hxb, wgt, ALU.mult))
            link(eng.tensor_copy(dst[:, :, :, 0:W1], prod))
            link(eng.tensor_tensor(rest, prod, dst[:, :, :, 0:W1], ALU.subtract))
            link(eng.tensor_copy(dst[:, :, :, W1:2 * W1], rest))
            link(eng.tensor_tensor(prod, rest, dst[:, :, :, W1:2 * W1], ALU.subtract))
            return eng.tensor_copy(dst[:, :, :, 2 * W1:3 * W1], prod)

        with nc.Block() as block:

            @block.sync
            def _(sp):
                def load_hx(head, q, bit):
                    a = bit % 2
                    c = head * NG + NB * q + bit
                    sp.wait_ge(xy_ready, c + 1)
                    sp.dma_start(hx[:, a, :, 0:DH], h_group[q, bit, head]).then_inc(hx_loaded[a], 16)

                def step_loads(head, q, bit):
                    a = bit % 2
                    n = head * NIB + NB * q + bit
                    blk = NB * q + bit
                    sp.wait_ge(b_ready, NG * n + 1)
                    sp.dma_start(s_bc[:, a, :], s_blk[head, blk].partition_broadcast(P))\
                      .then_inc(s_loaded[a], 16)
                    sp.wait_ge(result_ready, n + 1)
                    sp.dma_start(x_res[:, a, :, :], x_blk[blk, head]).then_inc(xr_loaded[a], 16)

                sp.wait_ge(hx_ones, 1)
                for q in range(NQG):
                    for bit in range(NB):
                        load_hx(0, q, bit)
                with sp.Fori(0, H - 1) as head:
                    with sp.Fori(0, NQG) as q:
                        for bit in range(NB):
                            step_loads(head, q, bit)
                            load_hx(head + 1, q, bit)
                with sp.Fori(0, NQG) as q:
                    for bit in range(NB):
                        step_loads(H - 1, q, bit)

            @block.gpsimd
            def _(pool):
                for s, k in ((c_ready, SLOTS), (groups_done, SLOTS), (xy_ready, 2), (acc_free, 2), (b_ready, NG + 1),
                             (result_ready, 2)):
                    pool.nop().then_inc(s, k)
                pool.memset(hx[:, :, :, DH:W1], 1.0).then_inc(hx_ones, 1)
                pool.wait_ge(hx_ones, 1)
                linked = Count(pool, "pool_linked", 1)
                heads_before = Count(pool, "heads_before", SLOTS, NG * NIB)

                def link(ins):
                    ins.then_inc(pool_chain, 1)
                    linked.wait(pool_chain)

                def chunk(head, at, q, bit):
                    a = bit % 2
                    c = head * NG + NB * q + bit
                    pool.wait_ge(hx_loaded[a], 16 * (head * (NG // 2) + 2 * q + bit // 2 + 1))
                    parts(pool, link, at, head, NB * q + bit, a).then_inc(xy_ready, 1)
                    pool.wait_ge(xy_ready, c + 1 + 2)

                def store(head, q, bit):
                    a = bit % 2
                    n = head * NIB + NB * q + bit
                    pool.wait_ge(result_ready, n + 3)
                    pool.dma_start(out_blk[NB * q + bit, head], o_sb[:, a, :, :]).then_inc(out_stored[a], 16)

                def head_steps(head, at):
                    with pool.Fori(0, NQG) as q:
                        for bit in range(NB):
                            chunk(head + 1, at, q, bit)
                            store(head, q, bit)

                pool.wait_ge(xy_ready, NG + 2)
                with pool.Fori(0, (H - 2) // 2) as pair:
                    for a in range(2):
                        heads_before.wait(groups_done)
                        head_steps(2 * pair + a, 1 - a)
                pool.wait_ge(groups_done, NG * NIB * (H - 2) + SLOTS)
                head_steps(H - 2, 1)
                with pool.Fori(0, NQG) as q:
                    for bit in range(NB):
                        store(H - 1, q, bit)
                for a in range(2):
                    pool.wait_ge(out_stored[a], 16 * (STEPS // 2))

            @block.tensor
            def _(pe):
                masks = Count(pe, "masks", NG + 2)

                def step(head, pair, hp, a):
                    n = head * NIB + 2 * pair + a
                    pe.wait_ge(acc_free, n + 1)
                    for g in range(NG):
                        slot = g % SLOTS
                        if a == 0:
                            pe.wait_ge(xy_ready, head * NG + g + 1 + 2)
                        masks.wait(b_ready)
                        for k in range(GK):
                            for t in range(IT):
                                for c, mask in enumerate((mask_b, mask_c)):
                                    last = nc.tensor.matmul(
                                        acc(a, t)[:, c, :],
                                        mask[:, slot, k, t * P:(t + 1) * P].bitcast(FP8),
                                        xy[:, hp, GK * g + k, c, :],
                                        start=(g == 0 and k == 0 and c == 0),
                                        stop=(g == NG - 1 and k == GK - 1 and c == 1),
                                        skip_group_check=True)
                        last.then_inc(groups_done, 1)

                with pe.Fori(0, H // 2) as heads:
                    for hp in range(2):
                        with pe.Fori(0, NIB // 2) as pair:
                            for a in range(2):
                                step(2 * heads + hp, pair, hp, a)

            @block.scalar
            def _(act):
                def low(n, a):
                    act.wait_ge(groups_done, NG * n + SLOTS)
                    act.wait_ge(acc_free, n + 1)
                    act.activation(low_parts, accs(a)[:, :, :, W1:MW], ACT.Copy).then_inc(low_copied, 1)

                slot_free = Count(act, "slot_free", 1)

                with act.Fori(0, H) as head:
                    with act.Fori(0, NIB // 2) as pair:
                        for a in range(2):
                            half = head * (NIB // 2) + pair
                            n = 2 * half + a
                            act.wait_ge(s_loaded[a], 16 * (half + 1))
                            for g in range(NG):
                                q, bit = divmod(g, NB)
                                slot_free.wait(c_ready)
                                for k in range(SIGNS):
                                    jt = NB * (GK * q + k) + bit
                                    last = act.activation(sgn[:, g % SLOTS, k, :], s_bc[:, a, :], ACT.Sign,
                                                          bias=t_sb[:, bass.ds(head, 1), jt])
                                last.then_inc(signs, 1)
                                if g == 2:
                                    if a == 0:
                                        with act.If(n > 0):
                                            low(n, 1)
                                    else:
                                        low(n, 0)
                low(STEPS, 1)

            @block.vector
            def _(dve):
                linked = Count(dve, "linked2", 1)
                o_free = [Count(dve, f"o_free{a}", 16, 16) for a in range(2)]
                signed = Count(dve, "signed", 1)
                masked = Count(dve, "masked", 1)
                cut = Count(dve, "cut", 1 + SLOTS)

                def link(ins):
                    ins.then_inc(chain2, 1)
                    linked.wait(chain2)

                for g in range(NG):
                    dve.wait_ge(hx_loaded[g % 2], 16 * (g // 2 + 1))
                    parts(dve, link, 0, 0, g, g % 2).then_inc(xy_ready, 1)
                    dve.wait_ge(xy_ready, g + 1 + 2)

                def rows(n, a, loaded, reused):
                    if reused is True:
                        o_free[a].wait(out_stored[a])
                    else:
                        with dve.If(reused):
                            o_free[a].wait(out_stored[a])
                    dve.wait_ge(low_copied, n)
                    link(dve.tensor_tensor(total, accs(a)[:, :, :, 0:W1], low_parts[:, :, :, 0:W1], ALU.add))
                    dve.tensor_tensor(total, total, low_parts[:, :, :, W1:2 * W1], ALU.add)\
                       .then_inc(acc_free, 1)
                    dve.wait_ge(acc_free, n + 2)
                    rows_coef = coef[:, bass.ds(n * IT, IT), :].unsqueeze(3)
                    link(dve.tensor_tensor(scaled, total, rows_coef.broadcast_to([P, IT, 2, W1]), ALU.mult))
                    link(dve.tensor_tensor(both, scaled[:, :, 0, :], scaled[:, :, 1, :], ALU.add))
                    link(dve.tensor_scalar(rden, both[:, :, DH], 1e-37, None, ALU.max))
                    link(dve.reciprocal(rden, rden))
                    link(dve.tensor_tensor(both[:, :, 0:DH], both[:, :, 0:DH],
                                           rden.unsqueeze(2).broadcast_to([P, IT, DH]), ALU.mult))
                    dve.wait_ge(xr_loaded[a], loaded)
                    dve.tensor_tensor(o_sb[:, a, :, :], both[:, :, 0:DH], x_res[:, a, :, :], ALU.add)\
                       .then_inc(result_ready, 1)

                with dve.Fori(0, H) as head:
                    with dve.Fori(0, NIB // 2) as pair:
                        for a in range(2):
                            half = head * (NIB // 2) + pair
                            n = 2 * half + a
                            dve.wait_ge(s_loaded[a], 16 * (half + 1))
                            for g in range(NG):
                                q, bit = divmod(g, NB)
                                slot = g % SLOTS
                                for k in range(SIGNS, GK):
                                    jt = NB * (GK * q + k) + bit
                                    last = dve.tensor_scalar(sgn[:, slot, k, :], s_bc[:, a, :],
                                                             neg_t[:, bass.ds(head, 1), jt], -1.0,
                                                             ALU.is_lt, ALU.mult)
                                link(last)
                                edges = packed[:, GK * q:GK * q + GK, bass.ds((2 * pair + a) * IB, IB)].bitcast(I32)
                                c_out = mask_c[:, slot, :, :].bitcast(I32)
                                signed.wait(signs)
                                masked.wait(groups_done)
                                word = BITS[bit] * 0x01010101
                                dve.scalar_tensor_tensor(c_out, sgn[:, slot, :, :].bitcast(I32), word, edges,
                                                         ALU.bitwise_and, ALU.bitwise_and).then_inc(c_ready, 1)
                                cut.wait(c_ready)
                                dve.scalar_tensor_tensor(mask_b[:, slot, :, :].bitcast(I32), edges, word, c_out,
                                                         ALU.bitwise_and, ALU.bitwise_xor).then_inc(b_ready, 1)
                                if g == 3:
                                    if a == 0:
                                        with dve.If(n > 0):
                                            rows(n, 1, 16 * half, half > 1)
                                    else:
                                        rows(n, 0, 16 * half + 16, half > 0)
                rows(STEPS, 1, 16 * (STEPS // 2), True)


_INS = ("x", "adj", "L0_gnn_W", "L0_gnn_b", "L0_gnn_aw")


def kernel(**inputs):
    import numpy as np
    import concourse.bacc as bacc
    from concourse.bass_utils import run_bass_kernel_spmd

    nc = bacc.Bacc("TRN2", target_bir_lowering=False, num_devices=1)
    arrays, args = {}, []
    for name in _INS:
        a = np.ascontiguousarray(inputs[name])
        arrays[f"in_{name}"] = a
        args.append(nc.dram_tensor(f"in_{name}", a.shape, mybir.dt.from_np(a.dtype), kind="ExternalInput").ap())
    h_dram = nc.dram_tensor("h_scratch", (N, F), F32).ap()
    s_dram = nc.dram_tensor("s_scratch", (H, N), F32).ap()
    out = nc.dram_tensor("out", (N, F), F32, kind="ExternalOutput").ap()
    gat_kernel(nc, *args, h_dram, s_dram, out)
    r = run_bass_kernel_spmd(nc, [arrays], core_ids=[0])
    return r.results[0]["out"]
```

```python
import concourse.bass as bass
from concourse import mybir
from contextlib import ExitStack

F32 = mybir.dt.float32
BF16 = mybir.dt.bfloat16
FP8 = mybir.dt.float8e4
I32 = mybir.dt.int32
I8 = mybir.dt.int8
U8 = mybir.dt.uint8
ALU = mybir.AluOpType
ACT = mybir.ActivationFunctionType
AX = mybir.AxisListType


P = 128
N = 6144
F = 512
H = 8
DH = 64
ALPHA = 0.2
EPS = 1e-5
NT = N // P
BITS = (0x40, 0x20, 0x10, 0x08)
BIT_INVERSE = (0.5, 8.0, 32.0, 64.0)
NB = len(BITS)
NQ = NT // NB
IB = 1024
IT = IB // P
NIB = N // IB
GK = 4
NG = NT // GK
NQG = NQ // GK
W1 = DH + 1
KC = F // P
SIGN_SLOTS = 3
SLOTS = 4
PAIR = 2
NPAIR = IT // PAIR
HEADROOM = 86
NEAR_ROOM = 5
NEAR_SPREAD = 12.0
NEAR_H = 16.0
LOW_BITS = 11
SIGNS = 3


class Plan:

    def __init__(self, parts, dtype, heads_held):
        self.parts, self.dtype, self.heads_held = parts, dtype, heads_held
        self.width = parts * W1


WIDE = Plan(3, BF16, 1)
NEAR = Plan(2, mybir.dt.float16, 2)


class Count:

    def __init__(self, eng, name, first, by=1):
        self.eng = eng
        self.by = by
        self.reg = eng.alloc_register(name)
        eng.reg_mov(self.reg, first)

    def wait(self, sem):
        self.eng.wait_ge(sem, self.reg)
        self.eng.reg_add(self.reg, self.reg, self.by)


def gat_kernel(nc, x, adj, w, b, aw, h_dram, s_dram, out):
    ctx = ExitStack()
    with ctx:
        def sb(name, shape, dt):
            return ctx.enter_context(nc.sbuf_tensor(name, shape, dt))

        def ps(name, shape, dt):
            return ctx.enter_context(nc.psum_tensor(name, shape, dt))

        def sem(name):
            return ctx.enter_context(nc.semaphore(name))

        packed = sb("packed", [P, NQ, N], U8)
        t_sb = sb("t_sb", [P, H, NT], F32)
        neg_t = sb("neg_t", [P, H, NT], F32)
        coef = sb("coef", [P, IT + H * NT, 2], F32)
        wxy = sb("wxy", [P, H * NT, 2], F32)
        flag = sb("flag", [P, 1], I32)

        ARENA = 32400
        arena = sb("arena", [P, ARENA], F32)

        def layout():
            at = [0]

            def carve(words, parts=P):
                at[0] += words
                assert at[0] <= ARENA, at[0]
                return arena[0:parts, at[0] - words:at[0]]
            return carve

        carve = layout()
        adj_raw = carve(2 * N).bitcast(I32).rearrange("p (a n) -> p a n", a=2)
        adj01 = carve(N).bitcast(BF16).rearrange("p (a n) -> p a n", a=2)
        w_nat = carve(KC * F).rearrange("p (c f) -> p c f", c=KC)
        wt = carve(KC * F).rearrange("p (k n) -> p k n", k=KC)
        x_in = carve(2 * F).rearrange("p (a f) -> p a f", a=2)
        xn = carve(2 * F).rearrange("p (a f) -> p a f", a=2)
        hn_t = carve(2 * F).rearrange("p (a k i) -> p a k i", a=2, k=KC)
        h_sb = carve(2 * F).rearrange("p (a f) -> p a f", a=2)
        b_bc = carve(F)
        b_rep = carve(KC * P).rearrange("p (c m) -> p c m", c=KC)
        ident = carve(P)
        ident_bits = carve(NB * P // 2).bitcast(BF16).rearrange("p (b m) -> p b m", b=NB)
        wa = carve(KC * 2 * H).rearrange("p (k m) -> p k m", k=KC)
        ba = carve(2 * H)
        aw_blk = carve(KC * 2 * H).rearrange("p (c m) -> p c m", c=KC)
        b_col = carve(KC)
        st_cols = carve(2 * H * (NT + 1)).rearrange("p (m t) -> p m t", t=NT + 1)
        st_all = st_cols[:, :, 1:NT + 1]
        stats = carve(2 * 6).rearrange("p (a m) -> p a m", a=2)
        mv = carve(2 * 2).rearrange("p (a m) -> p a m", a=2)
        ve = carve(2)
        std = carve(2)
        r0 = carve(2)
        r1 = carve(2)
        rstd = carve(2)
        h_abs = carve(NT + 1)
        extremes = carve(2 * H + 1)
        top = carve(2 * H + 1)
        spread = carve(H)
        over = carve(2)
        tmp = [w_nat[:, c, 0:H * NT] for c in range(KC)]
        s_t = wt[0:NT, :, :].rearrange("r k n -> r (k n)")[:, 0:H * P].rearrange("r (h i) -> r h i", h=H)

        psum = ps("psum", [P, 8, 512], F32)

        x_rows = x.rearrange("(t p) f -> t p f", p=P)
        adj_rows = adj.rearrange("(t p) j -> t p j", p=P)
        h_rows = h_dram.rearrange("(t p) f -> t p f", p=P)
        h_group = h_dram.rearrange("(g k b p) (h d) -> g b h p k d", p=P, b=NB, k=GK, d=DH)
        x_blk = x.rearrange("(n t p) (h d) -> n h p t d", p=P, t=IT, d=DH)
        out_blk = out.rearrange("(n t p) (h d) -> n h p t d", p=P, t=IT, d=DH)
        s_blk = s_dram.rearrange("h (n i) -> h n i", i=IB)

        w_in = sem("w_in")
        aw_in = sem("aw_in")
        x_loaded = [sem(f"x_loaded{a}") for a in range(2)]
        adj_loaded = [sem(f"adj_loaded{a}") for a in range(2)]
        ident_ready = sem("ident_ready")
        aw_zero = sem("aw_zero")
        brep_ready = sem("brep_ready")
        wt_ps = sem("wt_ps")
        wt_copied = sem("wt_copied")
        wa_ps = sem("wa_ps")
        wa_copied = sem("wa_copied")
        ve_ready = sem("ve_ready")
        std_ready = sem("std_ready")
        xn_ready = sem("xn_ready")
        adj01_ready = sem("adj01_ready")
        pack_done = sem("pack_done")
        pack_copied = sem("pack_copied")
        xt_done = sem("xt_done")
        hnt_ready = sem("hnt_ready")
        h_done = sem("h_done")
        h_ready = sem("h_ready")
        h_stored = [sem(f"h_stored{a}") for a in range(2)]
        chain1 = sem("chain1")
        tmax_ready = sem("tmax_ready")
        top_ready = sem("top_ready")
        arg_ready = sem("arg_ready")
        exp_ready = sem("exp_ready")
        st_ready = sem("st_ready")
        s_ps = sem("s_ps")
        s_copied = sem("s_copied")
        s_stored = sem("s_stored")
        wxy_ready = sem("wxy_ready")
        START = {"xn": 2, "adj01": 2, "pack": 2, "xt": 2, "hnt": 1, "h_done": 2, "h_ready": 1,
                 "pack_copied": 1}

        with nc.Block() as block:

            @block.sync
            def _(sp):
                sp.dma_start(w_nat, w.rearrange("(c p) f -> p c f", p=P)).then_inc(w_in, 16)
                sp.dma_start(b_bc, b.partition_broadcast(P)).then_inc(w_in, 16)
                sp.dma_start(b_col, b.rearrange("(c p) -> p c", p=P), allow_slow_non_contiguous=True).then_inc(w_in, 16)
                with sp.Fori(0, NT // 2) as i:
                    for a in range(2):
                        n = 2 * i + a
                        sp.wait_ge(xn_ready, n + 1)
                        sp.dma_start(x_in[:, a, :], x_rows[n]).then_inc(x_loaded[a], 16)
                        sp.wait_ge(adj01_ready, n + 1)
                        sp.dma_start(adj_raw[:, a, :], adj_rows[n]).then_inc(adj_loaded[a], 16)
                sp.wait_ge(s_copied, 1)
                sp.dma_start(s_dram.rearrange("h (r i) -> r h i", i=P), s_t).then_inc(s_stored, 16)
                sp.wait_ge(s_stored, 16)

            @block.gpsimd
            def _(pool):
                for s, count in ((xn_ready, START["xn"]), (adj01_ready, START["adj01"]),
                                 (pack_done, START["pack"]), (xt_done, START["xt"]),
                                 (hnt_ready, START["hnt"]), (h_done, START["h_done"]),
                                 (h_ready, START["h_ready"]), (pack_copied, START["pack_copied"])):
                    pool.nop().then_inc(s, count)
                pool.memset(aw_blk, 0.0).then_inc(aw_zero, 1)
                pool.memset(ident, 0.0).then_inc(aw_zero, 1)
                pool.wait_ge(aw_zero, 2)
                pool.affine_select(out=ident, in_=ident, compare_op=ALU.not_equal, fill=1.0, base=0,
                                   pattern=[[-1, P]], channel_multiplier=1).then_inc(ident_ready, 1)
                for h in range(H):
                    lo = (h % 2) * DH
                    pool.dma_start(aw_blk[lo:lo + DH, h // 2, h:h + H + 1:H], aw[h], allow_slow_non_contiguous=True).then_inc(aw_in, 16)
                with pool.Fori(0, NT // 2) as i:
                    for a in range(2):
                        n = 2 * i + a
                        pool.wait_ge(h_ready, n + 1 + START["h_ready"])
                        pool.dma_start(h_rows[n], h_sb[:, a, :]).then_inc(h_stored[a], 16)
                pool.wait_ge(tmax_ready, 1)
                pool.partition_all_reduce(top, extremes, P, bass.bass_isa.ReduceOp.max).then_inc(top_ready, 1)
                for a in range(2):
                    pool.wait_ge(h_stored[a], 16 * (NT // 2))

            @block.tensor
            def _(pe):
                ps_t = psum[:, 3, :].rearrange("p (k i) -> p k i", k=KC)
                ps_h = psum[:, 4, :]
                ps_st = psum[:, 5, 0:2 * H]
                ps_ba = psum[:, 6, 0:2 * H]
                pe.wait_ge(w_in, 48)
                pe.wait_ge(ident_ready, 1)
                for k in range(KC):
                    if k:
                        pe.wait_ge(wt_copied, k)
                    for c in range(KC):
                        last = nc.tensor.transpose(ps_t[:, c, :], w_nat[:, c, k * P:(k + 1) * P], ident)
                    last.then_inc(wt_ps, 1)
                pe.wait_ge(aw_in, 16 * H)
                pe.wait_ge(brep_ready, 1)
                for k in range(KC):
                    if k:
                        pe.wait_ge(wa_copied, k)
                    for c in range(KC):
                        last = nc.tensor.matmul(ps_st, w_nat[:, c, k * P:(k + 1) * P], aw_blk[:, c, :],
                                                start=(c == 0), stop=(c == KC - 1))
                    last.then_inc(wa_ps, 1)
                for c in range(KC):
                    last = nc.tensor.matmul(ps_ba, b_rep[:, c, :], aw_blk[:, c, :],
                                            start=(c == 0), stop=(c == KC - 1))
                last.then_inc(wa_ps, 1)
                pe.wait_ge(wa_copied, KC + 1)
                pe.wait_ge(wt_copied, KC)

                def pack(a, q):
                    bank, at = q // 4, (q % 4) * P
                    for bit in range(NB):
                        jt = NB * q + bit
                        last = nc.tensor.matmul(psum[:, bank, at:at + P],
                                                adj01[:, a, jt * P:(jt + 1) * P], ident_bits[:, bit, :],
                                                start=(bit == 0), stop=(bit == NB - 1))
                    return last

                with pe.Fori(0, NT // 2) as i:
                    for a in range(2):
                        n = 2 * i + a
                        pe.wait_ge(adj01_ready, n + 1 + START["adj01"])
                        pe.wait_ge(pack_copied, n + START["pack_copied"])
                        for q in range(NQ // 2):
                            pack(a, q)
                        pe.wait_ge(xn_ready, n + 1 + START["xn"])
                        pe.wait_ge(hnt_ready, n + START["hnt"])
                        for k in range(KC):
                            last = nc.tensor.transpose(ps_t[:, k, :], xn[:, a, k * P:(k + 1) * P], ident)
                        last.then_inc(xt_done, 1)
                        for q in range(NQ // 2, NQ):
                            last = pack(a, q)
                        last.then_inc(pack_done, 1)
                        pe.wait_ge(hnt_ready, n + 1 + START["hnt"])
                        pe.wait_ge(h_ready, n + START["h_ready"])
                        for k in range(KC):
                            nc.tensor.matmul(ps_h, hn_t[:, a, k, :], wt[:, k, :],
                                             start=(k == 0), stop=(k == KC - 1))
                        for k in range(KC):
                            last = nc.tensor.matmul(ps_st, hn_t[:, a, k, :], wa[:, k, :],
                                                    start=(k == 0), stop=(k == KC - 1))
                        last.then_inc(h_done, 1)
                pe.wait_ge(st_ready, 1)
                for h in range(H):
                    last = nc.tensor.transpose(psum[0:NT, 6 + h // 4, (h % 4) * P:(h % 4 + 1) * P],
                                               st_all[:, h, :], ident)
                last.then_inc(s_ps, 1)

            @block.scalar
            def _(act):
                for k in range(KC):
                    act.wait_ge(wt_ps, k + 1)
                    act.activation(wt[:, k, :], psum[:, 3, :], ACT.Copy).then_inc(wt_copied, 1)
                with act.Fori(0, NT // 2) as i:
                    for a in range(2):
                        n = 2 * i + a
                        act.wait_ge(ve_ready, n + 1)
                        act.activation(std[:, a:a + 1], ve[:, a:a + 1], ACT.Sqrt).then_inc(std_ready, 1)
                        act.wait_ge(h_done, n + START["h_done"] - 1)
                        act.wait_ge(xt_done, n + 1 + START["xt"])
                        act.activation(hn_t[:, a, :, :], psum[:, 3, :].rearrange("p (k i) -> p k i", k=KC),
                                       ACT.Relu).then_inc(hnt_ready, 1)
                        act.wait_ge(pack_done, n + 1 + START["pack"])
                        act.activation(packed[:, :, bass.ts(n, P)],
                                       psum[:, 0:3, :].rearrange("p k (q i) -> p (k q) i", q=4),
                                       ACT.Copy).then_inc(pack_copied, 1)
                t_less_top = wt[:, 2, 0:H * NT]
                for k, (arg, by) in enumerate(((tmp[0], 1.0), (tmp[1], 0.5), (t_less_top, 0.5),
                                               (t_less_top, ALPHA))):
                    act.wait_ge(arg_ready, min(k + 1, 3))
                    act.activation(tmp[k], arg, ACT.Exp, scale=by).then_inc(exp_ready, 1)

            @block.vector
            def _(dve):
                linked = Count(dve, "linked1", 1)
                h_free = [Count(dve, f"h_free{a}", 16, 16) for a in range(2)]

                def link(ins):
                    ins.then_inc(chain1, 1)
                    linked.wait(chain1)

                dve.wait_ge(w_in, 48)
                dve.tensor_copy(b_rep, b_col.unsqueeze(2).broadcast_to([P, KC, P])).then_inc(brep_ready, 1)
                dve.wait_ge(ident_ready, 1)
                for bit in range(NB):
                    link(dve.tensor_scalar(ident_bits[:, bit, :], ident, float(BITS[bit]), None, ALU.mult))
                for k in range(KC):
                    dve.wait_ge(wa_ps, k + 1)
                    dve.tensor_copy(wa[:, k, :], psum[:, 5, 0:2 * H]).then_inc(wa_copied, 1)
                dve.wait_ge(wa_ps, KC + 1)
                dve.tensor_copy(ba, psum[:, 6, 0:2 * H]).then_inc(wa_copied, 1)
                dve.wait_ge(wa_copied, KC + 1)

                def rows(n, a, half):
                    dve.wait_ge(x_loaded[a], 16 * (half + 1))
                    link(dve.bn_stats(stats[:, a, :], x_in[:, a, :]))
                    link(dve.bn_aggr(mv[:, a, :], stats[:, a, :]))
                    dve.tensor_scalar(ve[:, a:a + 1], mv[:, a, 1:2], EPS, None, ALU.add).then_inc(ve_ready, 1)
                    dve.wait_ge(adj_loaded[a], 16 * (half + 1))
                    dve.wait_ge(pack_done, n + START["pack"] - 1)
                    dve.tensor_scalar(adj01[:, a, :], adj_raw[:, a, :], 0.0, None, ALU.is_gt)\
                       .then_inc(adj01_ready, 1)
                    dve.wait_ge(std_ready, n + 1)
                    link(dve.reciprocal(r0[:, a:a + 1], std[:, a:a + 1]))
                    link(dve.scalar_tensor_tensor(r1[:, a:a + 1], r0[:, a:a + 1], ve[:, a:a + 1],
                                                  r0[:, a:a + 1], ALU.mult, ALU.mult))
                    link(dve.tensor_scalar(r1[:, a:a + 1], r1[:, a:a + 1], -0.5, 1.5, ALU.mult, ALU.add))
                    link(dve.tensor_tensor(rstd[:, a:a + 1], r0[:, a:a + 1], r1[:, a:a + 1], ALU.mult))
                    dve.wait_ge(xt_done, n + START["xt"] - 1)
                    dve.tensor_scalar(xn[:, a, :], x_in[:, a, :], mv[:, a, 0:1], rstd[:, a:a + 1],
                                      ALU.subtract, ALU.mult).then_inc(xn_ready, 1)

                def finish(m_plus_1, a, reused):
                    if reused is True:
                        h_free[a].wait(h_stored[a])
                    else:
                        with dve.If(reused):
                            h_free[a].wait(h_stored[a])
                    dve.wait_ge(h_done, m_plus_1 + START["h_done"])
                    link(dve.tensor_tensor(h_sb[:, a, :], psum[:, 4, :], b_bc, ALU.add))
                    link(dve.tensor_reduce(h_abs[:, bass.ds(m_plus_1, 1)], h_sb[:, a, :], AX.X, ALU.max,
                                           apply_absolute_value=True))
                    dve.tensor_tensor(st_cols[:, :, bass.ds(m_plus_1, 1)], psum[:, 5, 0:2 * H].unsqueeze(2),
                                      ba.unsqueeze(2), ALU.add).then_inc(h_ready, 1)

                with dve.Fori(0, NT // 2) as i:
                    for a in range(2):
                        n = 2 * i + a
                        rows(n, a, i)
                        if a == 0:
                            with dve.If(i > 0):
                                finish(n, 1, i > 1)
                        else:
                            finish(n, 0, i > 0)
                finish(NT, 1, True)

                dve.wait_ge(h_ready, NT + START["h_ready"])
                dve.nop().then_inc(st_ready, 1)
                s_all = st_all[:, 0:H, :]
                t_all = st_all[:, H:2 * H, :]
                link(dve.tensor_copy(t_sb[:, :, :], t_all))
                link(dve.tensor_scalar(neg_t[:, :, :], t_all, -1.0, None, ALU.mult))
                link(dve.tensor_reduce(extremes[:, 0:H], t_all, AX.X, ALU.max))
                link(dve.tensor_reduce(extremes[:, H:2 * H], neg_t[:, :, :], AX.X, ALU.max))
                dve.tensor_reduce(extremes[:, 2 * H:2 * H + 1], h_abs[:, 1:NT + 1], AX.X, ALU.max)\
                   .then_inc(tmax_ready, 1)
                dve.wait_ge(top_ready, 1)
                t_top = top[:, 0:H].unsqueeze(2).broadcast_to([P, H, NT])
                link(dve.tensor_tensor(spread, top[:, 0:H], top[:, H:2 * H], ALU.add))
                link(dve.tensor_reduce(over[:, 0:1], spread, AX.X, ALU.max))
                link(dve.tensor_scalar(over[:, 0:1], over[:, 0:1], NEAR_SPREAD, None, ALU.is_gt))
                link(dve.tensor_scalar(over[:, 1:2], top[:, 2 * H:2 * H + 1], NEAR_H, None, ALU.is_gt))
                link(dve.tensor_tensor(flag[:, :], over[:, 0:1], over[:, 1:2], ALU.max))
                v = [t.rearrange("p (h t) -> p h t", h=H) for t in tmp]
                z, guard = (wt[:, c, 0:H * NT].rearrange("p (h t) -> p h t", h=H) for c in range(2, 4))
                link(dve.tensor_tensor(z, s_all, t_top, ALU.add))
                link(dve.scalar_tensor_tensor(guard, z, ALPHA, z, ALU.mult, ALU.max))
                dve.tensor_tensor(v[0], z, guard, ALU.subtract).then_inc(arg_ready, 1)
                dve.wait_ge(arg_ready, 1)
                dve.scalar_tensor_tensor(v[1], z, ALPHA, guard, ALU.mult, ALU.subtract).then_inc(arg_ready, 1)
                dve.wait_ge(arg_ready, 2)
                dve.tensor_tensor(z, t_all, t_top, ALU.subtract).then_inc(arg_ready, 1)
                dve.wait_ge(s_ps, 1)
                dve.tensor_copy(s_t, psum[0:NT, 6:8, :].rearrange("r k (h i) -> r (k h) i", h=4))\
                   .then_inc(s_copied, 1)
                dve.wait_ge(s_copied, 1)
                coef_v = coef[:, IT:IT + H * NT, :].rearrange("p (h t) c -> p h t c", h=H)
                wxy_v = wxy[:, :, :].rearrange("p (h g b k) c -> p h g b k c", h=H, g=NQG, b=NB)
                half_room = float(2.0 ** (HEADROOM // 2))
                dve.wait_ge(exp_ready, 1)
                link(dve.tensor_copy(coef_v[:, :, :, 0], v[0]))
                dve.wait_ge(exp_ready, 2)
                link(dve.tensor_scalar(v[1], v[1], half_room, None, ALU.mult))
                link(dve.tensor_tensor(coef_v[:, :, :, 1], v[1], v[1], ALU.mult))
                dve.wait_ge(exp_ready, 3)
                link(dve.tensor_scalar(v[2], v[2], half_room, None, ALU.mult))
                link(dve.tensor_tensor(v[2], v[2], v[2], ALU.mult))
                dve.wait_ge(exp_ready, 4)
                for c in range(2):
                    in_order = v[2 + c].rearrange("p h (g k b) -> p h g b k", g=NQG, b=NB)
                    for bit in range(NB):
                        for g in range(NQG):
                            dve.tensor_scalar(wxy_v[:, :, g, bit, :, c], in_order[:, :, g, bit, :],
                                              BIT_INVERSE[bit], None, ALU.mult).then_inc(wxy_ready, 1)
                dve.wait_ge(wxy_ready, 2 * NB * NQG)

        s_loaded = [sem(f"s_loaded{a}") for a in range(2)]
        xr_loaded = [sem(f"xr_loaded{a}") for a in range(2)]
        hx_loaded = [sem(f"hx_loaded{a}") for a in range(2)]
        out_stored = [sem(f"out_stored{a}") for a in range(2)]
        hx_ones = sem("hx_ones")
        scales_set = sem("scales_set")
        signs = sem("signs")
        compares = sem("compares")
        c_ready = sem("c_ready")
        b_ready = sem("b_ready")
        groups_done = sem("groups_done")
        pair_done = sem("pair_done")
        pair_copied = sem("pair_copied")
        sums_read = sem("sums_read")
        xy_ready = sem("xy_ready")
        result_ready = sem("result_ready")
        rows_scaled = sem("rows_scaled")
        kinds_added = sem("kinds_added")
        inverted = sem("inverted")
        divided = sem("divided")
        chain2 = sem("chain2")
        pool_chain = sem("pool_chain")
        STEPS = H * NIB

        def attention(plan):
            MW, HELD = plan.width, plan.heads_held
            near = plan is NEAR
            carve = layout()
            xy = carve(HELD * NT * MW).bitcast(plan.dtype).rearrange("p (a t c m) -> p a t c m", a=HELD, t=NT, c=2)
            sgn, mask_b, mask_c = (carve(slots * GK * IB // 4).bitcast(I8)
                                   .rearrange("p (s k i) -> p s k i", s=slots, k=GK)
                                   for slots in (SIGN_SLOTS, SLOTS, SLOTS))
            s_bc = carve(2 * IB).rearrange("p (a i) -> p a i", a=2)
            hx = carve(2 * GK * W1).rearrange("p (a k m) -> p a k m", a=2, k=GK)
            prod = carve(GK * 2 * W1).rearrange("p (k c m) -> p k c m", k=GK, c=2)
            rest = carve(GK * 2 * W1).rearrange("p (k c m) -> p k c m", k=GK, c=2)
            sums = carve(IT * 2 * MW).rearrange("p (t c m) -> p t c m", t=IT, c=2)
            total = carve(IT * 2 * W1).rearrange("p (t c m) -> p t c m", t=IT, c=2)
            rden = carve(IT)
            low_scale = carve(1)
            x_out = carve(2 * IT * DH).rearrange("p (a t d) -> p a t d", a=2, t=IT)
            both = total[:, :, 0, :]

            def cut(eng, link, at, head, q, bit):
                g = NB * q + bit
                wgt = wxy[:, bass.ds(head * NT + GK * g, GK), :].unsqueeze(3).broadcast_to([P, GK, 2, W1])
                rows = hx[:, bit % 2, :, :].unsqueeze(2).broadcast_to([P, GK, 2, W1])
                dst = xy[:, at, bass.ds(GK * g, GK), :, :]
                high, low = dst[:, :, :, 0:W1], dst[:, :, :, W1:2 * W1]
                link(eng.tensor_tensor(prod, rows, wgt, ALU.mult))
                link(eng.tensor_copy(high, prod))
                link(eng.tensor_tensor(rest, prod, high, ALU.subtract))
                if near:
                    by = low_scale.unsqueeze(1).unsqueeze(1).broadcast_to([P, GK, 2, W1])
                    return eng.tensor_tensor(low, rest, by, ALU.mult)
                link(eng.tensor_copy(low, rest))
                link(eng.tensor_tensor(prod, rest, low, ALU.subtract))
                return eng.tensor_copy(dst[:, :, :, 2 * W1:3 * W1], prod)

            def sync_program(sp):
                def load_hx(head, q, bit):
                    sp.wait_ge(xy_ready, head * NG + NB * q + bit + 1)
                    sp.dma_start(hx[:, bit % 2, :, 0:DH], h_group[q, bit, head]).then_inc(hx_loaded[bit % 2], 16)

                def step_loads(head, blk, a, half):
                    n = head * NIB + blk
                    sp.wait_ge(b_ready, NG * n + 1)
                    sp.dma_start(s_bc[:, a, :], s_blk[head, blk].partition_broadcast(P))\
                      .then_inc(s_loaded[a], 16)

                    def load_x():
                        sp.dma_start(x_out[:, a, :, :], x_blk[blk, head]).then_inc(xr_loaded[a], 16)

                    if isinstance(head, int):
                        sp.wait_ge(out_stored[a], 16 * half)
                        load_x()
                    else:
                        with sp.If(half > 0):
                            sp.wait_ge(out_stored[a], 16 * half)
                            load_x()
                        with sp.If(half < 1):
                            load_x()

                def head_loads(head, with_next):
                    with sp.Fori(0, NIB // 2) as q:
                        for a in range(2):
                            step_loads(head, 2 * q + a, a, head * (NIB // 2) + q)
                            if with_next and HELD == 2:
                                for bit in (2 * a, 2 * a + 1):
                                    load_hx(head + 1, q, bit)
                    if with_next and HELD == 1:
                        with sp.Fori(0, NQG) as q:
                            for bit in range(NB):
                                load_hx(head + 1, q, bit)

                sp.wait_ge(hx_ones, 2)
                for q in range(NQG):
                    for bit in range(NB):
                        load_hx(0, q, bit)
                with sp.Fori(0, H - 1) as head:
                    head_loads(head, True)
                head_loads(H - 1, False)

            def gpsimd_program(pool):
                for s, k in ((c_ready, SIGN_SLOTS), (groups_done, SLOTS), (xy_ready, 2), (b_ready, NG + 1),
                             (pair_done, NPAIR - 1), (pair_copied, NPAIR), (sums_read, 1),
                             (result_ready, 2)):
                    pool.nop().then_inc(s, k)
                pool.memset(hx[:, :, :, DH:W1], 1.0).then_inc(hx_ones, 1)
                pool.memset(low_scale, float(2 ** LOW_BITS)).then_inc(hx_ones, 1)
                pool.wait_ge(hx_ones, 2)
                linked = Count(pool, f"pool_linked{MW}", 1)
                freed = Count(pool, f"xy_freed{MW}", SLOTS, NG * NIB)

                def link(ins):
                    ins.then_inc(pool_chain, 1)
                    linked.wait(pool_chain)

                def chunk(head, at, q, bit):
                    c = head * NG + NB * q + bit
                    if HELD == 1:
                        pool.wait_ge(groups_done, NG * (NIB * head - 1) + NB * q + bit + 1 + SLOTS)
                    pool.wait_ge(hx_loaded[bit % 2], 16 * (head * (NG // 2) + 2 * q + bit // 2 + 1))
                    cut(pool, link, at, head, q, bit).then_inc(xy_ready, 1)
                    pool.wait_ge(xy_ready, c + 1 + 2)

                def store(head, blk, a):
                    n = head * NIB + blk
                    pool.wait_ge(result_ready, n + 3)
                    pool.dma_start(out_blk[blk, head], x_out[:, a, :, :]).then_inc(out_stored[a], 16)

                pool.wait_ge(xy_ready, NG + 2)
                if HELD == 2:
                    def beside(head, at):
                        with pool.Fori(0, NIB // 2) as q:
                            for a in range(2):
                                for bit in (2 * a, 2 * a + 1):
                                    chunk(head + 1, at, q, bit)
                                store(head, 2 * q + a, a)

                    with pool.Fori(0, (H - 2) // 2) as two:
                        for a in range(2):
                            freed.wait(groups_done)
                            beside(2 * two + a, 1 - a)
                    pool.wait_ge(groups_done, NG * NIB * (H - 2) + SLOTS)
                    beside(H - 2, 1)
                else:
                    with pool.Fori(0, H - 1) as head:
                        for blk in range(NIB - 1):
                            store(head, blk, blk % 2)
                        with pool.Fori(0, NQG) as q:
                            for bit in range(NB):
                                chunk(head + 1, 0, q, bit)
                        store(head, NIB - 1, 1)
                for blk in range(NIB):
                    store(H - 1, blk, blk % 2)
                for a in range(2):
                    pool.wait_ge(out_stored[a], 16 * (STEPS // 2))

            def tensor_program(pe):
                masks = Count(pe, f"masks{MW}", NG + 2)
                banks = Count(pe, f"banks{MW}", 1)

                def step(head, at):
                    for g in range(NG):
                        pe.wait_ge(xy_ready, head * NG + g + 1 + 2)
                        masks.wait(b_ready)
                        for t in range(IT):
                            if g == 0 and t % PAIR == 0:
                                banks.wait(pair_copied)
                            for k in range(GK):
                                for c, mask in enumerate((mask_b, mask_c)):
                                    last = nc.tensor.matmul(
                                        psum[:, t, c * MW:(c + 1) * MW],
                                        mask[:, g % SLOTS, k, t * P:(t + 1) * P].bitcast(FP8),
                                        xy[:, at, GK * g + k, c, :],
                                        start=(g == 0 and k == 0 and c == 0),
                                        stop=(g == NG - 1 and k == GK - 1 and c == 1),
                                        skip_group_check=True)
                            if g == NG - 1 and t % PAIR == PAIR - 1 and t < IT - 1:
                                last.then_inc(pair_done, 1)
                        last.then_inc(groups_done, 1)

                with pe.Fori(0, H // HELD) as heads:
                    for at in range(HELD):
                        with pe.Fori(0, NIB):
                            step(HELD * heads + at, at)

            def scalar_program(act):
                slot_free = Count(act, f"slot_free{MW}", 1)

                def copy_sums(n):
                    act.wait_ge(sums_read, n)
                    for p in range(NPAIR):
                        if p < NPAIR - 1:
                            act.wait_ge(pair_done, (NPAIR - 1) * n + p + 1)
                        else:
                            act.wait_ge(groups_done, NG * n + SLOTS)
                        act.activation(sums[:, PAIR * p:PAIR * p + PAIR, :, :],
                                       psum[:, PAIR * p:PAIR * p + PAIR, 0:2 * MW]
                                       .rearrange("p t (c m) -> p t c m", c=2), ACT.Copy)\
                           .then_inc(pair_copied, 1)

                with act.Fori(0, H) as head:
                    with act.Fori(0, NIB // 2) as two:
                        for a in range(2):
                            half = head * (NIB // 2) + two
                            act.wait_ge(s_loaded[a], 16 * (half + 1))
                            for g in range(NG):
                                q, bit = divmod(g, NB)
                                slot_free.wait(c_ready)
                                for k in range(SIGNS):
                                    jt = NB * (GK * q + k) + bit
                                    last = act.activation(sgn[:, g % SIGN_SLOTS, k, :], s_bc[:, a, :], ACT.Sign,
                                                          bias=t_sb[:, bass.ds(head, 1), jt])
                                last.then_inc(signs, 1)
                                if g == 2:
                                    if a == 0:
                                        with act.If(half > 0):
                                            copy_sums(2 * half)
                                    else:
                                        copy_sums(2 * half + 1)
                copy_sums(STEPS)

            def vector_program(dve):
                linked = Count(dve, f"linked{MW}", 1)
                compared = Count(dve, f"compared{MW}", 1)
                signed = Count(dve, f"signed{MW}", 1)
                masked = Count(dve, f"masked{MW}", 1)
                cut_c = Count(dve, f"cut_c{MW}", 1 + SIGN_SLOTS)

                def link(ins):
                    ins.then_inc(chain2, 1)
                    linked.wait(chain2)

                if near:
                    for table, by in ((wxy[:, :, 0], 2.0 ** (NEAR_ROOM - HEADROOM)),
                                      (wxy[:, :, 1], 2.0 ** NEAR_ROOM),
                                      (coef[:, IT:IT + H * NT, 1], 2.0 ** -HEADROOM)):
                        dve.tensor_scalar(table, table, by, None, ALU.mult).then_inc(scales_set, 1)
                    dve.wait_ge(scales_set, 3)
                for g in range(NG):
                    dve.wait_ge(hx_loaded[g % 2], 16 * (g // 2 + 1))
                    cut(dve, link, 0, 0, g // NB, g % NB).then_inc(xy_ready, 1)
                    dve.wait_ge(xy_ready, g + 1 + 2)

                def add_parts(n, a, loaded):
                    dve.wait_ge(pair_copied, NPAIR * n + NPAIR)
                    high, low = sums[:, :, :, 0:W1], sums[:, :, :, W1:2 * W1]
                    if near:
                        dve.scalar_tensor_tensor(total, low, 2.0 ** -LOW_BITS, high, ALU.mult, ALU.add)\
                           .then_inc(sums_read, 1)
                    else:
                        link(dve.tensor_tensor(total, sums[:, :, :, 2 * W1:3 * W1], low, ALU.add))
                        dve.tensor_tensor(total, total, high, ALU.add).then_inc(sums_read, 1)

                def scale_rows(n, a, loaded):
                    dve.wait_ge(sums_read, n + 1)
                    rows_coef = coef[:, bass.ds(n * IT, IT), :].unsqueeze(3)
                    dve.tensor_tensor(total, total, rows_coef.broadcast_to([P, IT, 2, W1]), ALU.mult)\
                       .then_inc(rows_scaled, 1)

                def add_kinds(n, a, loaded):
                    dve.wait_ge(rows_scaled, n)
                    dve.tensor_tensor(both, total[:, :, 0, :], total[:, :, 1, :], ALU.add)\
                       .then_inc(kinds_added, 1)

                def invert(n, a, loaded):
                    dve.wait_ge(kinds_added, n)
                    link(dve.tensor_scalar(rden, both[:, :, DH], 1e-37, None, ALU.max))
                    dve.reciprocal(rden, rden).then_inc(inverted, 1)

                def divide(n, a, loaded):
                    dve.wait_ge(inverted, n)
                    dve.tensor_tensor(both[:, :, 0:DH], both[:, :, 0:DH],
                                      rden.unsqueeze(2).broadcast_to([P, IT, DH]), ALU.mult).then_inc(divided, 1)

                def add_x(n, a, loaded):
                    dve.wait_ge(divided, n)
                    dve.wait_ge(xr_loaded[a], loaded)
                    dve.tensor_tensor(x_out[:, a, :, :], both[:, :, 0:DH], x_out[:, a, :, :], ALU.add)\
                       .then_inc(result_ready, 1)

                PIECES = (add_parts, scale_rows, add_kinds, invert, divide, add_x)
                FIRST_PIECE = 3

                with dve.Fori(0, H) as head:
                    with dve.Fori(0, NIB // 2) as two:
                        for a in range(2):
                            half = head * (NIB // 2) + two
                            n = 2 * half + a
                            dve.wait_ge(s_loaded[a], 16 * (half + 1))

                            def compare(g):
                                q, bit = divmod(g, NB)
                                for k in range(SIGNS, GK):
                                    jt = NB * (GK * q + k) + bit
                                    last = dve.tensor_scalar(sgn[:, g % SIGN_SLOTS, k, :], s_bc[:, a, :],
                                                             neg_t[:, bass.ds(head, 1), jt], -1.0,
                                                             ALU.is_lt, ALU.mult)
                                last.then_inc(compares, 1)

                            compare(0)
                            for g in range(NG):
                                q, bit = divmod(g, NB)
                                slot = g % SLOTS
                                edges = packed[:, GK * q:GK * q + GK, bass.ds((2 * two + a) * IB, IB)].bitcast(I32)
                                c_out = mask_c[:, slot, :, :].bitcast(I32)
                                compared.wait(compares)
                                signed.wait(signs)
                                masked.wait(groups_done)
                                word = BITS[bit] * 0x01010101
                                dve.scalar_tensor_tensor(c_out, sgn[:, g % SIGN_SLOTS, :, :].bitcast(I32), word, edges,
                                                         ALU.bitwise_and, ALU.bitwise_and).then_inc(c_ready, 1)
                                if g + 1 < NG:
                                    compare(g + 1)
                                cut_c.wait(c_ready)
                                dve.scalar_tensor_tensor(mask_b[:, slot, :, :].bitcast(I32), edges, word, c_out,
                                                         ALU.bitwise_and, ALU.bitwise_xor).then_inc(b_ready, 1)
                                if FIRST_PIECE <= g < FIRST_PIECE + len(PIECES):
                                    piece = PIECES[g - FIRST_PIECE]
                                    if a == 0:
                                        with dve.If(half > 0):
                                            piece(n, 1, 16 * half)
                                    else:
                                        piece(n, 0, 16 * half + 16)
                for piece in PIECES:
                    piece(STEPS, 1, 16 * (STEPS // 2))

            return sync_program, gpsimd_program, tensor_program, scalar_program, vector_program

        wide, near = attention(WIDE), attention(NEAR)

        with nc.Block() as block:
            def chosen(eng, which):
                is_wide = eng.value_load(flag[0:1, 0:1], min_val=0, max_val=1)
                with eng.If(is_wide > 0):
                    wide[which](eng)
                with eng.If(is_wide < 1):
                    near[which](eng)

            @block.sync
            def _(sp):
                chosen(sp, 0)

            @block.gpsimd
            def _(pool):
                chosen(pool, 1)

            @block.tensor
            def _(pe):
                chosen(pe, 2)

            @block.scalar
            def _(act):
                chosen(act, 3)

            @block.vector
            def _(dve):
                chosen(dve, 4)


_INS = ("x", "adj", "L0_gnn_W", "L0_gnn_b", "L0_gnn_aw")


def kernel(**inputs):
    import numpy as np
    import concourse.bacc as bacc
    from concourse.bass_utils import run_bass_kernel_spmd

    nc = bacc.Bacc("TRN2", target_bir_lowering=False, num_devices=1)
    arrays, args = {}, []
    for name in _INS:
        a = np.ascontiguousarray(inputs[name])
        arrays[f"in_{name}"] = a
        args.append(nc.dram_tensor(f"in_{name}", a.shape, mybir.dt.from_np(a.dtype), kind="ExternalInput").ap())
    h_dram = nc.dram_tensor("h_scratch", (N, F), F32).ap()
    s_dram = nc.dram_tensor("s_scratch", (H, N), F32).ap()
    out = nc.dram_tensor("out", (N, F), F32, kind="ExternalOutput").ap()
    gat_kernel(nc, *args, h_dram, s_dram, out)
    r = run_bass_kernel_spmd(nc, [arrays], core_ids=[0])
    return r.results[0]["out"]
```

```python
import concourse.bass as bass
from concourse import mybir
from contextlib import ExitStack, nullcontext

F32 = mybir.dt.float32
BF16 = mybir.dt.bfloat16
FP8 = mybir.dt.float8e4
I32 = mybir.dt.int32
I8 = mybir.dt.int8
U8 = mybir.dt.uint8
ALU = mybir.AluOpType
ACT = mybir.ActivationFunctionType
AX = mybir.AxisListType


P = 128
N = 6144
F = 512
H = 8
DH = 64
ALPHA = 0.2
EPS = 1e-5
NT = N // P
BITS = (0x40, 0x20, 0x10, 0x08)
BIT_INVERSE = (0.5, 8.0, 32.0, 64.0)
NB = len(BITS)
NQ = NT // NB
IB = 1024
IT = IB // P
NIB = N // IB
GK = 4
NG = NT // GK
NQG = NQ // GK
W1 = DH + 1
KC = F // P
SIGN_SLOTS = 3
SLOTS = 4
NT1 = NT // 2
NH2 = 2 * (NT - NT1)
PC = 1024
NPC = N // 2 // PC
CUTS = 1
PACK_STEPS = NH2 // NG
COMPARE_LAG = 1
COPY_LAG = 4
COPIES0 = 2 * COPY_LAG + 1
HEADROOM = 86
NEAR_ROOM = 5
NEAR_SPREAD = 12.0
NEAR_H = 16.0
LOW_BITS = 11
SIGNS = 3


class Plan:

    def __init__(self, parts, dtype, heads_held, banks):
        self.parts, self.dtype, self.heads_held = parts, dtype, heads_held
        self.width = parts * W1
        self.place, self.copies = [], []
        bank = 0
        for count, units in banks:
            self.copies.append((bank, count, units, len(self.place)))
            self.place += [(bank + u // units, u % units) for u in range(count * units)]
            bank += count
        self.first_tile = [first // 2 for _, _, _, first in self.copies]
        self.last_tile = [(first + count * units - 1) // 2 for _, count, units, first in self.copies]


WIDE = Plan(3, BF16, 1, [(2, 2)] * 4)
NEAR = Plan(2, mybir.dt.float16, 2, [(1, 3)] * 4 + [(2, 2)])


class Count:

    def __init__(self, eng, name, first, by=1):
        self.eng = eng
        self.by = by
        self.reg = eng.alloc_register(name)
        eng.reg_mov(self.reg, first)

    def wait(self, sem):
        self.eng.wait_ge(sem, self.reg)
        self.eng.reg_add(self.reg, self.reg, self.by)


def gat_kernel(nc, x, adj, w, b, aw, h_dram, s_dram, out):
    ctx = ExitStack()
    with ctx:
        def sb(name, shape, dt):
            return ctx.enter_context(nc.sbuf_tensor(name, shape, dt))

        def ps(name, shape, dt):
            return ctx.enter_context(nc.psum_tensor(name, shape, dt))

        def sem(name):
            return ctx.enter_context(nc.semaphore(name))

        packed = sb("packed", [P, NQ, N], U8)
        t_sb = sb("t_sb", [P, H, NT], F32)
        neg_t = sb("neg_t", [P, H, NT], F32)
        coef = sb("coef", [P, IT + H * NT, 2], F32)
        wxy = sb("wxy", [P, H * NT, 2], F32)
        flag = sb("flag", [P, 1], I32)

        ident_bits = sb("ident_bits", [P, NB, P], BF16)

        ARENA = 32128
        arena = sb("arena", [P, ARENA], F32)

        def layout():
            at = [0]

            def carve(words, parts=P):
                at[0] += words
                assert at[0] <= ARENA, at[0]
                return arena[0:parts, at[0] - words:at[0]]
            return carve

        carve = layout()
        adj_raw = carve(2 * N).bitcast(I32).rearrange("p (a n) -> p a n", a=2)
        adj01 = carve(N).bitcast(BF16).rearrange("p (a n) -> p a n", a=2)
        w_nat = carve(KC * F).rearrange("p (c f) -> p c f", c=KC)
        wt = carve(KC * F).rearrange("p (k n) -> p k n", k=KC)
        x_in = carve(2 * 2 * F).rearrange("p (a e f) -> p a e f", a=2, e=2)
        xn = carve(2 * F).rearrange("p (a f) -> p a f", a=2)
        hn_t = carve(2 * F).rearrange("p (a k i) -> p a k i", a=2, k=KC)
        h_sb = carve(2 * F).rearrange("p (a f) -> p a f", a=2)
        b_bc = carve(F)
        b_rep = carve(KC * P).rearrange("p (c m) -> p c m", c=KC)
        ident = carve(P)
        wa = carve(KC * 2 * H).rearrange("p (k m) -> p k m", k=KC)
        ba = carve(2 * H)
        aw_blk = carve(KC * 2 * H).rearrange("p (c m) -> p c m", c=KC)
        b_col = carve(KC)
        st_cols = carve(2 * H * (NT + 2)).rearrange("p (m t) -> p m t", t=NT + 2)
        st_all = st_cols[:, :, 2:NT + 2]
        stats = carve(2 * 6).rearrange("p (a m) -> p a m", a=2)
        mv = carve(2 * 2).rearrange("p (a m) -> p a m", a=2)
        ve = carve(2)
        std = carve(2)
        r0 = carve(2)
        r1 = carve(2)
        rstd = carve(2)
        h_abs = carve(NT + 2)
        extremes = carve(2 * H + 1)
        top = carve(2 * H + 1)
        spread = carve(H)
        over = carve(2)
        tmp = [w_nat[:, c, 0:H * NT] for c in range(KC)]
        s_t = wt[0:NT, :, :].rearrange("r k n -> r (k n)")[:, 0:H * P].rearrange("r (h i) -> r h i", h=H)

        carve = layout()
        carve(NT * NEAR.width)
        piece_raw = carve(NPC * PC).bitcast(I32).rearrange("p (j n) -> p j n", j=NPC)
        piece01 = carve(2 * NPC * PC // 2).bitcast(BF16).rearrange("p (a j n) -> p a j n", a=2, j=NPC)
        assert NPC * PC * 2 <= NT * NEAR.width

        psum = ps("psum", [P, 8, 512], F32)

        x_pairs = x.rearrange("(m e p) f -> m p e f", e=2, p=P)
        adj_rows = adj.rearrange("(t p) j -> t p j", p=P)
        h_rows = h_dram.rearrange("(t p) f -> t p f", p=P)
        h_group = h_dram.rearrange("(g k b p) (h d) -> g b h p k d", p=P, b=NB, k=GK, d=DH)
        x_blk = x.rearrange("(n t p) (h d) -> n h p t d", p=P, t=IT, d=DH)
        out_blk = out.rearrange("(n t p) (h d) -> n h p t d", p=P, t=IT, d=DH)
        s_blk = s_dram.rearrange("h (n i) -> h n i", i=IB)

        w_in = sem("w_in")
        aw_in = sem("aw_in")
        x_loaded = [sem(f"x_loaded{a}") for a in range(2)]
        adj_loaded = [sem(f"adj_loaded{a}") for a in range(2)]
        ident_ready = sem("ident_ready")
        aw_zero = sem("aw_zero")
        ident_zero = sem("ident_zero")
        brep_ready = sem("brep_ready")
        wt_ps = sem("wt_ps")
        wt_copied = sem("wt_copied")
        wa_ps = sem("wa_ps")
        wa_copied = sem("wa_copied")
        ve_ready = sem("ve_ready")
        std_ready = sem("std_ready")
        xn_ready = sem("xn_ready")
        adj01_ready = sem("adj01_ready")
        pack_done = sem("pack_done")
        pack_copied = sem("pack_copied")
        xt_done = sem("xt_done")
        hnt_ready = sem("hnt_ready")
        h_done = sem("h_done")
        h_ready = sem("h_ready")
        h_stored = [sem(f"h_stored{a}") for a in range(2)]
        stats_ready = sem("stats_ready")
        h_added = sem("h_added")
        h_maximum = sem("h_maximum")
        chain1 = sem("chain1")
        extremes_ready = sem("extremes_ready")
        top_ready = sem("top_ready")
        arg_ready = sem("arg_ready")
        exp_ready = sem("exp_ready")
        st_ready = sem("st_ready")
        s_ps = sem("s_ps")
        s_copied = sem("s_copied")
        s_stored = sem("s_stored")
        wxy_ready = sem("wxy_ready")
        START = {"xn": 4, "adj01": 2, "pack": 2, "xt": 2, "hnt": 1, "h_done": 2, "h_ready": 2, "h_maximum": 4,
                 "pack_copied": 1}

        with nc.Block() as block:

            @block.sync
            def _(sp):
                sp.dma_start(w_nat, w.rearrange("(c p) f -> p c f", p=P)).then_inc(w_in, 16)
                sp.dma_start(b_bc, b.partition_broadcast(P)).then_inc(w_in, 16)
                sp.dma_start(b_col, b.rearrange("(c p) -> p c", p=P), allow_slow_non_contiguous=True).then_inc(w_in, 16)
                with sp.Fori(0, NT1 // 2) as i:
                    for a in range(2):
                        m = 2 * i + a
                        sp.wait_ge(xn_ready, 2 * m + 2)
                        sp.dma_start(x_in[:, a, :, :], x_pairs[m]).then_inc(x_loaded[a], 16)
                        if a == 0:
                            sp.wait_ge(aw_in, 16 * H)
                        sp.wait_ge(adj01_ready, m + 1)
                        sp.dma_start(adj_raw[:, a, :], adj_rows[m]).then_inc(adj_loaded[a], 16)
                sp.wait_ge(s_copied, 1)
                sp.dma_start(s_dram.rearrange("h (r i) -> r h i", i=P), s_t).then_inc(s_stored, 16)
                sp.wait_ge(s_stored, 16)

            @block.gpsimd
            def _(pool):
                for s, count in ((xn_ready, START["xn"]), (adj01_ready, START["adj01"]),
                                 (pack_done, START["pack"]), (xt_done, START["xt"]),
                                 (hnt_ready, START["hnt"]), (h_done, START["h_done"]),
                                 (h_ready, START["h_ready"]), (pack_copied, START["pack_copied"]),
                                 (h_maximum, START["h_maximum"])):
                    pool.nop().then_inc(s, count)
                pool.memset(aw_blk, 0.0).then_inc(aw_zero, 1)
                pool.memset(ident, 0.0).then_inc(ident_zero, 1)
                pool.wait_ge(ident_zero, 1)
                pool.affine_select(out=ident, in_=ident, compare_op=ALU.not_equal, fill=1.0, base=0,
                                   pattern=[[-1, P]], channel_multiplier=1).then_inc(ident_ready, 1)
                with pool.Fori(0, NT // 2) as i:
                    for a in range(2):
                        n = 2 * i + a
                        pool.wait_ge(h_ready, n + 1 + START["h_ready"])
                        pool.dma_start(h_rows[n], h_sb[:, a, :]).then_inc(h_stored[a], 16)
                pool.wait_ge(extremes_ready, 1)
                pool.partition_all_reduce(top, extremes, P, bass.bass_isa.ReduceOp.max).then_inc(top_ready, 1)
                for a in range(2):
                    pool.wait_ge(h_stored[a], 16 * (NT // 2))

            @block.tensor
            def _(pe):
                ps_t = psum[:, 3, :].rearrange("p (k i) -> p k i", k=KC)
                ps_ba = psum[:, 7, 0:2 * H]
                pe.wait_ge(w_in, 48)
                pe.wait_ge(ident_ready, 1)
                for k in range(KC):
                    for c in range(KC):
                        last = nc.tensor.transpose(psum[:, k, c * P:(c + 1) * P], w_nat[:, c, k * P:(k + 1) * P], ident)
                    last.then_inc(wt_ps, 1)
                pe.wait_ge(aw_in, 16 * H)
                pe.wait_ge(brep_ready, 1)
                for k in range(KC):
                    for c in range(KC):
                        nc.tensor.matmul(psum[:, 6, 2 * H * k:2 * H * (k + 1)], w_nat[:, c, k * P:(k + 1) * P], aw_blk[:, c, :],
                                         start=(c == 0), stop=(c == KC - 1))
                for c in range(KC):
                    last = nc.tensor.matmul(ps_ba, b_rep[:, c, :], aw_blk[:, c, :],
                                            start=(c == 0), stop=(c == KC - 1))
                last.then_inc(wa_ps, 1)
                pe.wait_ge(wa_copied, 2)
                pe.wait_ge(wt_copied, KC)

                def pack(a, q):
                    bank, at = q // 4, (q % 4) * P
                    for bit in range(NB):
                        jt = NB * q + bit
                        last = nc.tensor.matmul(psum[:, bank, at:at + P],
                                                adj01[:, a, jt * P:(jt + 1) * P], ident_bits[:, bit, :],
                                                start=(bit == 0), stop=(bit == NB - 1))
                    return last

                def transpose_x(n, e):
                    pe.wait_ge(xn_ready, n + 1 + START["xn"])
                    pe.wait_ge(hnt_ready, n + START["hnt"])
                    for k in range(KC):
                        last = nc.tensor.transpose(ps_t[:, k, :], xn[:, e, k * P:(k + 1) * P], ident)
                    last.then_inc(xt_done, 1)

                def project(n, e):
                    pe.wait_ge(hnt_ready, n + 1 + START["hnt"])
                    pe.wait_ge(h_ready, n + START["h_ready"] - 1)
                    for k in range(KC):
                        nc.tensor.matmul(psum[:, 4 + e, :], hn_t[:, e, k, :], wt[:, k, :],
                                         start=(k == 0), stop=(k == KC - 1))
                    for k in range(KC):
                        last = nc.tensor.matmul(psum[:, 6 + e, 0:2 * H], hn_t[:, e, k, :], wa[:, k, :],
                                                start=(k == 0), stop=(k == KC - 1))
                    last.then_inc(h_done, 1)

                def project_pair(m):
                    for e in range(2):
                        project(2 * m + e, e)

                for e in range(2):
                    transpose_x(e, e)
                project_pair(0)
                more = NT1 // 2 - 1
                with pe.Fori(0, NT1 // 2) as i:
                    for a in range(2):
                        m = 2 * i + a
                        if a == 0:
                            transpose_x(2 * m + 2, 0)
                        else:
                            with pe.If(i < more):
                                transpose_x(2 * m + 2, 0)
                        pe.wait_ge(adj01_ready, m + 1 + START["adj01"])
                        pe.wait_ge(pack_copied, m + START["pack_copied"])
                        for q in range(NQ):
                            last = pack(a, q)
                        last.then_inc(pack_done, 1)
                        if a == 0:
                            transpose_x(2 * m + 3, 1)
                            project_pair(m + 1)
                        else:
                            with pe.If(i < more):
                                transpose_x(2 * m + 3, 1)
                                project_pair(m + 1)
                pe.wait_ge(st_ready, 1)
                for h in range(H):
                    last = nc.tensor.transpose(psum[0:NT, 6 + h // 4, (h % 4) * P:(h % 4 + 1) * P],
                                               st_all[:, h, :], ident)
                last.then_inc(s_ps, 1)

            @block.scalar
            def _(act):
                act.wait_ge(aw_zero, 1)
                for h in range(H):
                    lo = (h % 2) * DH
                    act.dma_start(aw_blk[lo:lo + DH, h // 2, h:h + H + 1:H], aw[h],
                                  allow_slow_non_contiguous=True).then_inc(aw_in, 16)
                for k in range(KC):
                    act.wait_ge(wt_ps, k + 1)
                    act.activation(wt[:, k, :], psum[:, k, :], ACT.Copy).then_inc(wt_copied, 1)

                def root(m):
                    act.wait_ge(ve_ready, m + 1)
                    act.activation(std, ve, ACT.Sqrt).then_inc(std_ready, 1)

                def rectify(m):
                    for e in range(2):
                        n = 2 * m + e
                        act.wait_ge(h_done, n + START["h_done"] - 1)
                        act.wait_ge(xt_done, n + 1 + START["xt"])
                        act.activation(hn_t[:, e, :, :], psum[:, 3, :].rearrange("p (k i) -> p k i", k=KC),
                                       ACT.Relu).then_inc(hnt_ready, 1)

                root(0)
                rectify(0)
                root(1)
                more = NT1 // 2 - 1
                with act.Fori(0, NT1 // 2) as i:
                    for a in range(2):
                        m = 2 * i + a
                        if a == 0:
                            rectify(m + 1)
                            with act.If(i < more):
                                root(m + 2)
                        else:
                            with act.If(i < more):
                                rectify(m + 1)
                                root(m + 2)
                        act.wait_ge(pack_done, m + 1 + START["pack"])
                        act.activation(packed[:, :, bass.ts(m, P)],
                                       psum[:, 0:3, :].rearrange("p k (q i) -> p (k q) i", q=4),
                                       ACT.Copy).then_inc(pack_copied, 1)
                t_less_top = wt[:, 2, 0:H * NT]
                for k, (arg, by) in enumerate(((tmp[0], 1.0), (tmp[1], 0.5), (t_less_top, 0.5),
                                               (t_less_top, ALPHA))):
                    act.wait_ge(arg_ready, min(k + 1, 3))
                    act.activation(tmp[k], arg, ACT.Exp, scale=by).then_inc(exp_ready, 1)

            @block.vector
            def _(dve):
                linked = Count(dve, "linked1", 1)
                stats_linked = Count(dve, "stats_linked", 1)
                added = Count(dve, "added", 1)
                h_free = [Count(dve, f"h_free{a}", 16, 16) for a in range(2)]

                def link(ins):
                    ins.then_inc(chain1, 1)
                    linked.wait(chain1)

                dve.wait_ge(w_in, 48)
                dve.tensor_copy(b_rep, b_col.unsqueeze(2).broadcast_to([P, KC, P])).then_inc(brep_ready, 1)
                dve.wait_ge(ident_ready, 1)
                for bit in range(NB):
                    link(dve.tensor_scalar(ident_bits[:, bit, :], ident, float(BITS[bit]), None, ALU.mult))
                def statistics(m, a, half):
                    dve.wait_ge(xn_ready, 2 * m + START["xn"])
                    dve.wait_ge(x_loaded[a], 16 * (half + 1))
                    for e in range(2):
                        dve.bn_stats(stats[:, e, :], x_in[:, a, e, :]).then_inc(stats_ready, 1)
                    for e in range(2):
                        stats_linked.wait(stats_ready)
                        dve.bn_aggr(mv[:, e, :], stats[:, e, :]).then_inc(chain1, 1)
                    for e in range(2):
                        linked.wait(chain1)
                    dve.tensor_scalar(ve, mv[:, :, 1], EPS, None, ALU.add).then_inc(ve_ready, 1)

                def normalise(m, a):
                    dve.wait_ge(std_ready, m + 1)
                    link(dve.reciprocal(r0, std))
                    link(dve.tensor_tensor(r1, r0, ve, ALU.mult))
                    link(dve.tensor_tensor(r1, r1, r0, ALU.mult))
                    link(dve.tensor_scalar(r1, r1, -0.5, 1.5, ALU.mult, ALU.add))
                    link(dve.tensor_tensor(rstd, r0, r1, ALU.mult))
                    for e in range(2):
                        dve.wait_ge(xt_done, 2 * m + e + START["xt"] - 1)
                        dve.tensor_scalar(xn[:, e, :], x_in[:, a, e, :], mv[:, e, 0:1], rstd[:, e:e + 1],
                                          ALU.subtract, ALU.mult).then_inc(xn_ready, 1)

                def compare_adj(m, a, half):
                    dve.wait_ge(adj_loaded[a], 16 * (half + 1))
                    dve.wait_ge(pack_done, m + START["pack"] - 1)
                    dve.tensor_scalar(adj01[:, a, :], adj_raw[:, a, :], 0.0, None, ALU.is_gt)\
                       .then_inc(adj01_ready, 1)

                def finish(after, reused):
                    for e in range(2):
                        if reused is True:
                            h_free[e].wait(h_stored[e])
                        else:
                            with dve.If(reused):
                                h_free[e].wait(h_stored[e])
                    for e in range(2):
                        dve.wait_ge(h_maximum, after + e + 1)
                        dve.wait_ge(h_done, after + e - 1 + START["h_done"])
                        dve.tensor_tensor(h_sb[:, e, :], psum[:, 4 + e, :], b_bc, ALU.add)\
                           .then_inc(h_added, 1)
                        dve.tensor_tensor(st_cols[:, :, bass.ds(after + e, 1)],
                                          psum[:, 6 + e, 0:2 * H].unsqueeze(2),
                                          ba.unsqueeze(2), ALU.add).then_inc(h_ready, 1)
                    for e in range(2):
                        added.wait(h_added)
                        dve.tensor_reduce(h_abs[:, bass.ds(after + e, 1)], h_sb[:, e, :], AX.X, ALU.max,
                                          apply_absolute_value=True).then_inc(h_maximum, 1)

                statistics(0, 0, 0)
                dve.wait_ge(wa_ps, 1)
                dve.tensor_copy(wa, psum[:, 6, 0:KC * 2 * H].rearrange("p (k m) -> p k m", k=KC))\
                   .then_inc(wa_copied, 1)
                dve.tensor_copy(ba, psum[:, 7, 0:2 * H]).then_inc(wa_copied, 1)
                dve.wait_ge(wa_copied, 2)
                with dve.Fori(0, NT1 // 2) as i:
                    for a in range(2):
                        m = 2 * i + a
                        normalise(m, a)
                        if a == 0:
                            with dve.If(i > 0):
                                finish(2 * m, True)
                        else:
                            finish(2 * m, i > 0)
                        if a == 0:
                            statistics(m + 1, 1, i)
                        else:
                            with dve.If(i < NT1 // 2 - 1):
                                statistics(m + 1, 0, i + 1)
                        compare_adj(m, a, i)
                finish(NT, True)

                dve.wait_ge(h_ready, NT + START["h_ready"])
                dve.wait_ge(h_maximum, NT + START["h_maximum"])
                dve.nop().then_inc(st_ready, 1)
                s_all = st_all[:, 0:H, :]
                t_all = st_all[:, H:2 * H, :]
                link(dve.tensor_copy(t_sb[:, :, :], t_all))
                link(dve.tensor_scalar(neg_t[:, :, :], t_all, -1.0, None, ALU.mult))
                link(dve.tensor_reduce(extremes[:, 0:H], t_all, AX.X, ALU.max))
                link(dve.tensor_reduce(extremes[:, H:2 * H], neg_t[:, :, :], AX.X, ALU.max))
                dve.tensor_reduce(extremes[:, 2 * H:2 * H + 1], h_abs[:, 2:NT + 2], AX.X, ALU.max)\
                   .then_inc(extremes_ready, 1)
                dve.wait_ge(top_ready, 1)
                t_top = top[:, 0:H].unsqueeze(2).broadcast_to([P, H, NT])
                link(dve.tensor_tensor(spread, top[:, 0:H], top[:, H:2 * H], ALU.add))
                link(dve.tensor_reduce(over[:, 0:1], spread, AX.X, ALU.max))
                link(dve.tensor_scalar(over[:, 0:1], over[:, 0:1], NEAR_SPREAD, None, ALU.is_gt))
                link(dve.tensor_scalar(over[:, 1:2], top[:, 2 * H:2 * H + 1], NEAR_H, None, ALU.is_gt))
                link(dve.tensor_tensor(flag[:, :], over[:, 0:1], over[:, 1:2], ALU.max))
                v = [t.rearrange("p (h t) -> p h t", h=H) for t in tmp]
                z, guard = (wt[:, c, 0:H * NT].rearrange("p (h t) -> p h t", h=H) for c in range(2, 4))
                link(dve.tensor_tensor(z, s_all, t_top, ALU.add))
                link(dve.scalar_tensor_tensor(guard, z, ALPHA, z, ALU.mult, ALU.max))
                dve.tensor_tensor(v[0], z, guard, ALU.subtract).then_inc(arg_ready, 1)
                dve.wait_ge(arg_ready, 1)
                dve.scalar_tensor_tensor(v[1], z, ALPHA, guard, ALU.mult, ALU.subtract).then_inc(arg_ready, 1)
                dve.wait_ge(arg_ready, 2)
                dve.tensor_tensor(z, t_all, t_top, ALU.subtract).then_inc(arg_ready, 1)
                dve.wait_ge(s_ps, 1)
                dve.tensor_copy(s_t, psum[0:NT, 6:8, :].rearrange("r k (h i) -> r (k h) i", h=4))\
                   .then_inc(s_copied, 1)
                dve.wait_ge(s_copied, 1)
                coef_v = coef[:, IT:IT + H * NT, :].rearrange("p (h t) c -> p h t c", h=H)
                wxy_v = wxy[:, :, :].rearrange("p (h g b k) c -> p h g b k c", h=H, g=NQG, b=NB)
                half_room = float(2.0 ** (HEADROOM // 2))
                dve.wait_ge(exp_ready, 1)
                link(dve.tensor_copy(coef_v[:, :, :, 0], v[0]))
                dve.wait_ge(exp_ready, 2)
                link(dve.tensor_scalar(v[1], v[1], half_room, None, ALU.mult))
                link(dve.tensor_tensor(coef_v[:, :, :, 1], v[1], v[1], ALU.mult))
                dve.wait_ge(exp_ready, 3)
                link(dve.tensor_scalar(v[2], v[2], half_room, None, ALU.mult))
                link(dve.tensor_tensor(v[2], v[2], v[2], ALU.mult))
                dve.wait_ge(exp_ready, 4)
                for c in range(2):
                    in_order = v[2 + c].rearrange("p h (g k b) -> p h g b k", g=NQG, b=NB)
                    for bit in range(NB):
                        dve.tensor_scalar(wxy_v[:, :, :, bit, :, c], in_order[:, :, :, bit, :],
                                          BIT_INVERSE[bit], None, ALU.mult).then_inc(wxy_ready, 1)
                dve.wait_ge(wxy_ready, 2 * NB)

        s_loaded = [sem(f"s_loaded{a}") for a in range(2)]
        xr_loaded = [sem(f"xr_loaded{a}") for a in range(2)]
        hx_loaded = [sem(f"hx_loaded{a}") for a in range(2)]
        out_stored = [sem(f"out_stored{a}") for a in range(2)]
        hx_ones = sem("hx_ones")
        scales_set = sem("scales_set")
        signs = sem("signs")
        compares = sem("compares")
        c_ready = sem("c_ready")
        b_ready = sem("b_ready")
        groups_done = sem("groups_done")
        sums_done = sem("sums_done")
        sums_copied = sem("sums_copied")
        piece_loaded = [sem(f"piece_loaded{j}") for j in range(NPC)]
        piece_ready = sem("piece_ready")
        half_packed = sem("half_packed")
        half_copied = sem("half_copied")
        sums_read = sem("sums_read")
        xy_ready = sem("xy_ready")
        result_ready = sem("result_ready")
        rows_scaled = sem("rows_scaled")
        kinds_added = sem("kinds_added")
        inverted = sem("inverted")
        divided = sem("divided")
        chain2 = sem("chain2")
        pool_chain = sem("pool_chain")
        STEPS = H * NIB

        def load_piece(sp, tile, half, j):
            lo = half * (N // 2) + j * PC
            sp.dma_start(piece_raw[:, j, :], adj_rows[tile][:, lo:lo + PC]).then_inc(piece_loaded[j], 16)

        def compare_piece(dve, half, j, packed_count, loaded_counts):
            if j == 0:
                packed_count.wait(half_packed)
            loaded_counts[j].wait(piece_loaded[j])
            dve.tensor_scalar(piece01[:, half, j, :], piece_raw[:, j, :], 0.0, None, ALU.is_gt)\
               .then_inc(piece_ready, 1)

        def compare_half(dve, half, packed_count, loaded_counts):
            for j in range(NPC):
                compare_piece(dve, half, j, packed_count, loaded_counts)

        def pack_half(pe, half, ready_count, copied_count):
            ready_count.wait(piece_ready)
            copied_count.wait(half_copied)
            for u in range(NQ // 2):
                j, v = divmod(u, PC // (NB * P))
                for bit in range(NB):
                    last = nc.tensor.matmul(psum[:, 6 + u // 3, (u % 3) * P:(u % 3 + 1) * P],
                                            piece01[:, half, j, (NB * v + bit) * P:(NB * v + bit + 1) * P],
                                            ident_bits[:, bit, :], start=(bit == 0), stop=(bit == NB - 1))
            last.then_inc(half_packed, 1)

        def copy_half(act, tile, half, count):
            count.wait(half_packed)
            act.activation(packed[:, 6 * half:6 * half + 6, bass.ds(tile * P, P)]
                           .rearrange("p (k q) i -> p k q i", k=2),
                           psum[:, 6:8, 0:3 * P].rearrange("p k (q i) -> p k q i", q=3),
                           ACT.Copy).then_inc(half_copied, 1)

        def attention(plan):
            MW, HELD = plan.width, plan.heads_held
            COPIES = len(plan.copies)
            near = plan is NEAR
            first_two = PACK_STEPS // 2
            carve = layout()
            xy = carve(HELD * NT * MW).bitcast(plan.dtype).rearrange("p (a t c m) -> p a t c m", a=HELD, t=NT, c=2)
            sgn, mask_b, mask_c = (carve(slots * GK * IB // 4).bitcast(I8)
                                   .rearrange("p (s k i) -> p s k i", s=slots, k=GK)
                                   for slots in (SIGN_SLOTS, SLOTS, SLOTS))
            s_bc = carve(2 * IB).rearrange("p (a i) -> p a i", a=2)
            hx = carve(2 * GK * W1).rearrange("p (a k m) -> p a k m", a=2, k=GK)
            prod = carve(GK * 2 * W1).rearrange("p (k c m) -> p k c m", k=GK, c=2)
            rest = carve(GK * 2 * W1).rearrange("p (k c m) -> p k c m", k=GK, c=2)
            sums = carve(IT * 2 * MW).rearrange("p (u m) -> p u m", u=2 * IT)
            total = carve(IT * 2 * W1).rearrange("p (u m) -> p u m", u=2 * IT)
            rows_of = total.rearrange("p (t c) m -> p t c m", c=2)
            rden = carve(IT)
            low_scale = carve(1)
            x_out = carve(2 * IT * DH).rearrange("p (a t d) -> p a t d", a=2, t=IT)
            both = rows_of[:, :, 0, :]

            def cut(eng, link, at, head, q, bit):
                g = NB * q + bit
                wgt = wxy[:, bass.ds(head * NT + GK * g, GK), :].unsqueeze(3).broadcast_to([P, GK, 2, W1])
                rows = hx[:, bit % 2, :, :].unsqueeze(2).broadcast_to([P, GK, 2, W1])
                dst = xy[:, at, bass.ds(GK * g, GK), :, :]
                high, low = dst[:, :, :, 0:W1], dst[:, :, :, W1:2 * W1]
                link(eng.tensor_tensor(prod, rows, wgt, ALU.mult))
                link(eng.tensor_copy(high, prod))
                link(eng.tensor_tensor(rest, prod, high, ALU.subtract))
                if near:
                    by = low_scale.unsqueeze(1).unsqueeze(1).broadcast_to([P, GK, 2, W1])
                    return eng.tensor_tensor(low, rest, by, ALU.mult)
                link(eng.tensor_copy(low, rest))
                link(eng.tensor_tensor(prod, rest, low, ALU.subtract))
                return eng.tensor_copy(dst[:, :, :, 2 * W1:3 * W1], prod)

            def sync_program(sp):
                def load_hx(head, q, bit):
                    sp.wait_ge(xy_ready, head * NG + NB * q + bit + 1)
                    sp.dma_start(hx[:, bit % 2, :, 0:DH], h_group[q, bit, head]).then_inc(hx_loaded[bit % 2], 16)

                def load_s(head, blk, a):
                    sp.wait_ge(b_ready, NG * (head * NIB + blk) + 1)
                    sp.dma_start(s_bc[:, a, :], s_blk[head, blk].partition_broadcast(P))\
                      .then_inc(s_loaded[a], 16)

                def load_x(head, blk, a, half):
                    def load():
                        sp.dma_start(x_out[:, a, :, :], x_blk[blk, head]).then_inc(xr_loaded[a], 16)

                    if isinstance(half, int):
                        if half:
                            sp.wait_ge(out_stored[a], 16 * half)
                        load()
                    else:
                        with sp.If(half > 0):
                            sp.wait_ge(out_stored[a], 16 * half)
                            load()
                        with sp.If(half < 1):
                            load()

                def load_half(tile, half):
                    for j in range(NPC):
                        sp.wait_ge(piece_ready, NPC * (2 * tile + half) + j + 1)
                        load_piece(sp, NT1 + tile, half, j)

                def load_tiles(lo, count):
                    with sp.Fori(0, count) as t:
                        load_half(lo + t, 1)
                        load_half(lo + t + 1, 0)

                def loads_beside(n):
                    lo = NG // 2 * n
                    load_tiles(lo, NG // 4)
                    load_s(0, n + 1, (n + 1) % 2)
                    load_tiles(lo + NG // 4, NG // 4 - 1)
                    load_x(0, n + 1, (n + 1) % 2, (n + 1) // 2)
                    load_half(lo + NG // 2 - 1, 1)
                    if n + 1 < PACK_STEPS:
                        load_half(lo + NG // 2, 0)

                def head_loads(head, with_next):
                    with sp.Fori(0, NIB // 2) as q:
                        for a in range(2):
                            if near and a == 0 and with_next:
                                with sp.If(head * NIB + q > NIB):
                                    load_s(head, 2 * q + a, a)
                            else:
                                load_s(head, 2 * q + a, a)
                            load_x(head, 2 * q + a, a, head * (NIB // 2) + q)
                            if with_next and HELD == 2:
                                for bit in (2 * a, 2 * a + 1):
                                    load_hx(head + 1, q, bit)
                    if with_next and HELD == 1:
                        with sp.Fori(0, NQG) as q:
                            for bit in range(NB):
                                load_hx(head + 1, q, bit)

                sp.wait_ge(hx_ones, 2)
                for c in range(2):
                    load_hx(0, 0, c)
                first_head = 0
                if near:
                    load_s(0, 0, 0)
                    load_x(0, 0, 0, 0)
                    for j in range(NPC):
                        load_piece(sp, NT1, 0, j)
                    for c in range(2, CUTS + 2):
                        load_hx(0, c // NB, c % NB)
                    for g in range(NG):
                        load_half((g + 1) // 2, (g + 1) % 2)
                        if CUTS + 2 + g < NG:
                            load_hx(0, (CUTS + 2 + g) // NB, (CUTS + 2 + g) % NB)
                        if g == NG // 2:
                            load_s(0, 1, 1)
                    load_x(0, 1, 1, 0)
                    for n in range(1, PACK_STEPS):
                        loads_beside(n)
                    for blk in range(PACK_STEPS, NIB):
                        if blk > PACK_STEPS:
                            load_s(0, blk, blk % 2)
                    for c in range(NG):
                        if c == NG // 2:
                            load_x(0, NIB - 1, 1, NIB // 2 - 1)
                        if c == NG - 4:
                            load_s(1, 0, 0)
                        load_hx(1, c // NB, c % NB)
                    first_head = 1
                else:
                    for c in range(2, NG):
                        load_hx(0, c // NB, c % NB)
                with sp.Fori(first_head, H - 1) as head:
                    head_loads(head, True)
                head_loads(H - 1, False)

            def gpsimd_program(pool):
                for s, k in ((c_ready, SIGN_SLOTS), (groups_done, SLOTS), (xy_ready, 2), (b_ready, NG + 1),
                             (sums_done, COPIES - 1), (sums_copied, COPIES), (sums_read, 1),
                             (result_ready, 2)):
                    pool.nop().then_inc(s, k)
                pool.memset(hx[:, :, :, DH:W1], 1.0).then_inc(hx_ones, 1)
                pool.memset(low_scale, float(2 ** LOW_BITS)).then_inc(hx_ones, 1)
                pool.wait_ge(hx_ones, 2)
                linked = Count(pool, f"pool_linked{MW}", 1)
                freed = Count(pool, f"xy_freed{MW}", SLOTS + NG * NIB, NG * NIB)

                def link(ins):
                    ins.then_inc(pool_chain, 1)
                    linked.wait(pool_chain)

                def chunk(head, at, q, bit):
                    c = head * NG + NB * q + bit
                    if HELD == 1:
                        pool.wait_ge(groups_done, NG * (NIB * head - 1) + NB * q + bit + 1 + SLOTS)
                    pool.wait_ge(hx_loaded[bit % 2], 16 * (head * (NG // 2) + 2 * q + bit // 2 + 1))
                    cut(pool, link, at, head, q, bit).then_inc(xy_ready, 1)
                    pool.wait_ge(xy_ready, c + 1 + 2)

                def store(head, blk, a):
                    n = head * NIB + blk
                    pool.wait_ge(result_ready, n + 3)
                    pool.dma_start(out_blk[blk, head], x_out[:, a, :, :]).then_inc(out_stored[a], 16)

                pool.wait_ge(xy_ready, (CUTS if near else NG) + 2)
                if near:
                    for c in range(CUTS, NG):
                        chunk(0, 0, c // NB, c % NB)
                if HELD == 2:
                    def beside(head, at):
                        with pool.Fori(0, NIB // 2) as q:
                            for a in range(2):
                                for bit in (2 * a, 2 * a + 1):
                                    chunk(head + 1, at, q, bit)
                                store(head, 2 * q + a, a)

                    for blk in range(PACK_STEPS - 1):
                        store(0, blk, blk % 2)
                    pool.wait_ge(half_copied, NH2 + COPIES0)
                    for c in range(NG):
                        chunk(1, 1, c // NB, c % NB)
                        if c % NB == NB - 1 and c < NG - 1:
                            store(0, PACK_STEPS - 1 + c // NB, (PACK_STEPS - 1 + c // NB) % 2)
                    store(0, NIB - 1, 1)
                    with pool.Fori(0, (H - 2) // 2) as two:
                        for a in range(2):
                            freed.wait(groups_done)
                            beside(2 * two + a + 1, a)
                else:
                    with pool.Fori(0, H - 1) as head:
                        for blk in range(NIB - 1):
                            store(head, blk, blk % 2)
                        with pool.Fori(0, NQG) as q:
                            for bit in range(NB):
                                chunk(head + 1, 0, q, bit)
                        store(head, NIB - 1, 1)
                for blk in range(NIB):
                    store(H - 1, blk, blk % 2)
                for a in range(2):
                    pool.wait_ge(out_stored[a], 16 * (STEPS // 2))

            def tensor_program(pe):
                masks = Count(pe, f"masks{MW}", NG + 2)
                banks = Count(pe, f"banks{MW}", 1)

                def step(head, at, packs=None):
                    for g in range(NG):
                        pe.wait_ge(xy_ready, head * NG + g + 1 + 2)
                        masks.wait(b_ready)
                        for t in range(IT):
                            if g == 0:
                                for first in plan.first_tile:
                                    if first == t:
                                        banks.wait(sums_copied)
                            for k in range(GK):
                                for c, mask in enumerate((mask_b, mask_c)):
                                    bank, unit = plan.place[2 * t + c]
                                    last = nc.tensor.matmul(
                                        psum[:, bank, unit * MW:(unit + 1) * MW],
                                        mask[:, g % SLOTS, k, t * P:(t + 1) * P].bitcast(FP8),
                                        xy[:, at, GK * g + k, c, :],
                                        start=(g == 0 and k == 0 and unit == 0),
                                        stop=(g == NG - 1 and k == GK - 1),
                                        skip_group_check=True)
                            if g == NG - 1 and t in plan.last_tile[:-1]:
                                last.then_inc(sums_done, 1)
                        last.then_inc(groups_done, 1)
                        if packs:
                            pack_half(pe, g % 2, *packs)

                if near:
                    packs = Count(pe, "pieces", 2 * NPC, NPC), Count(pe, "copies", COPIES0)
                    with pe.Fori(0, PACK_STEPS):
                        step(0, 0, packs)
                    start = pe.alloc_register("first_block")
                    pe.reg_mov(start, PACK_STEPS)
                    with pe.Fori(0, H // HELD) as heads:
                        for at in range(HELD):
                            with pe.Fori(start if at == 0 else 0, NIB):
                                step(HELD * heads + at, at)
                            if at == 0:
                                pe.reg_mov(start, 0)
                else:
                    with pe.Fori(0, H) as head:
                        with pe.Fori(0, NIB):
                            step(head, 0)

            def after_first(eng, half):
                return nullcontext() if isinstance(half, int) else eng.If(half > 0)

            def scalar_program(act):
                slot_free = Count(act, f"slot_free{MW}", 1)

                def copy_sums(n):
                    act.wait_ge(sums_read, n)
                    for p, (bank, count, units, first) in enumerate(plan.copies):
                        if p < COPIES - 1:
                            act.wait_ge(sums_done, (COPIES - 1) * n + p + 1)
                        else:
                            act.wait_ge(groups_done, NG * n + SLOTS)
                        act.activation(sums[:, first:first + count * units, :]
                                       .rearrange("p (b u) m -> p b (u m)", b=count),
                                       psum[:, bank:bank + count, 0:units * MW], ACT.Copy)\
                           .then_inc(sums_copied, 1)

                def step(head, half, a, copies=None):
                    behind = isinstance(half, int) and half == first_two
                    act.wait_ge(s_loaded[a], 16 * (half + 1))
                    for g in range(NG):
                        q, bit = divmod(g, NB)
                        slot_free.wait(c_ready)
                        for k in range(SIGNS):
                            jt = NB * (GK * q + k) + bit
                            last = act.activation(sgn[:, g % SIGN_SLOTS, k, :], s_bc[:, a, :], ACT.Sign,
                                                  bias=t_sb[:, bass.ds(head, 1), jt])
                        last.then_inc(signs, 1)
                        if copies and (not behind or g < COPY_LAG):
                            tile = NT1 + (NG // 2) * (2 * half + a) + (g - COPY_LAG) // 2
                            if g < COPY_LAG and a == 0:
                                with after_first(act, half):
                                    copy_half(act, tile, g % 2, copies)
                            else:
                                copy_half(act, tile, g % 2, copies)
                        if g == 2:
                            if a == 0:
                                with after_first(act, half):
                                    copy_sums(2 * half)
                            else:
                                copy_sums(2 * half + 1)

                if near:
                    copies = Count(act, "halves", 3)
                    with act.Fori(0, first_two) as two:
                        for a in range(2):
                            step(0, two, a, copies)
                    for two in range(first_two, NIB // 2):
                        for a in range(2):
                            step(0, two, a, copies if two == first_two and a == 0 else None)
                with act.Fori(1 if near else 0, H) as head:
                    with act.Fori(0, NIB // 2) as two:
                        for a in range(2):
                            step(head, head * (NIB // 2) + two, a)
                copy_sums(STEPS)

            def vector_program(dve):
                linked = Count(dve, f"linked{MW}", 1)
                compared = Count(dve, f"compared{MW}", 1)
                signed = Count(dve, f"signed{MW}", 1)
                masked = Count(dve, f"masked{MW}", 1)
                cut_c = Count(dve, f"cut_c{MW}", 1 + SIGN_SLOTS)

                def link(ins):
                    ins.then_inc(chain2, 1)
                    linked.wait(chain2)

                if near:
                    for table, by in ((wxy[:, :, 0], 2.0 ** (NEAR_ROOM - HEADROOM)),
                                      (wxy[:, :, 1], 2.0 ** NEAR_ROOM),
                                      (coef[:, IT:IT + H * NT, 1], 2.0 ** -HEADROOM)):
                        dve.tensor_scalar(table, table, by, None, ALU.mult).then_inc(scales_set, 1)
                    dve.wait_ge(scales_set, 3)
                for g in range(CUTS if near else NG):
                    dve.wait_ge(hx_loaded[g % 2], 16 * (g // 2 + 1))
                    cut(dve, link, 0, 0, g // NB, g % NB).then_inc(xy_ready, 1)
                    dve.wait_ge(xy_ready, g + 1 + 2)

                def add_parts(n, a, loaded):
                    dve.wait_ge(sums_copied, COPIES * n + COPIES)
                    high, low = sums[:, :, 0:W1], sums[:, :, W1:2 * W1]
                    if near:
                        dve.scalar_tensor_tensor(total, low, 2.0 ** -LOW_BITS, high, ALU.mult, ALU.add)\
                           .then_inc(sums_read, 1)
                    else:
                        link(dve.tensor_tensor(total, sums[:, :, 2 * W1:3 * W1], low, ALU.add))
                        dve.tensor_tensor(total, total, high, ALU.add).then_inc(sums_read, 1)

                def scale_rows(n, a, loaded):
                    dve.wait_ge(sums_read, n + 1)
                    rows_coef = coef[:, bass.ds(n * IT, IT), :].unsqueeze(3)
                    dve.tensor_tensor(rows_of, rows_of, rows_coef.broadcast_to([P, IT, 2, W1]), ALU.mult)\
                       .then_inc(rows_scaled, 1)

                def add_kinds(n, a, loaded):
                    dve.wait_ge(rows_scaled, n)
                    dve.tensor_tensor(both, rows_of[:, :, 0, :], rows_of[:, :, 1, :], ALU.add)\
                       .then_inc(kinds_added, 1)

                def invert(n, a, loaded):
                    dve.wait_ge(kinds_added, n)
                    link(dve.tensor_scalar(rden, both[:, :, DH], 1e-37, None, ALU.max))
                    dve.reciprocal(rden, rden).then_inc(inverted, 1)

                def divide(n, a, loaded):
                    dve.wait_ge(inverted, n)
                    dve.tensor_tensor(both[:, :, 0:DH], both[:, :, 0:DH],
                                      rden.unsqueeze(2).broadcast_to([P, IT, DH]), ALU.mult).then_inc(divided, 1)

                def add_x(n, a, loaded):
                    dve.wait_ge(divided, n)
                    dve.wait_ge(xr_loaded[a], loaded)
                    dve.tensor_tensor(x_out[:, a, :, :], both[:, :, 0:DH], x_out[:, a, :, :], ALU.add)\
                       .then_inc(result_ready, 1)

                PIECES = (add_parts, scale_rows, add_kinds, invert, divide, add_x)
                FIRST_PIECE = 3

                def step(head, blk, half, a, halves=None):
                    n = 2 * half + a
                    behind = isinstance(half, int) and half == first_two
                    dve.wait_ge(s_loaded[a], 16 * (half + 1))
                    if halves:
                        dve.wait_ge(half_copied, NG * n + COPIES0 - 2 * COPY_LAG)
                    if behind and a == 1:
                        dve.wait_ge(half_copied, NH2 + COPIES0)

                    def compare(g):
                        q, bit = divmod(g, NB)
                        for k in range(SIGNS, GK):
                            jt = NB * (GK * q + k) + bit
                            last = dve.tensor_scalar(sgn[:, g % SIGN_SLOTS, k, :], s_bc[:, a, :],
                                                     neg_t[:, bass.ds(head, 1), jt], -1.0,
                                                     ALU.is_lt, ALU.mult)
                        last.then_inc(compares, 1)

                    def piece_of_half(j):
                        if halves and (not behind or g < COMPARE_LAG):
                            if g < COMPARE_LAG and a == 0:
                                with after_first(dve, half):
                                    compare_piece(dve, (g - COMPARE_LAG) % 2, j, *halves)
                            else:
                                compare_piece(dve, (g - COMPARE_LAG) % 2, j, *halves)

                    compare(0)
                    for g in range(NG):
                        q, bit = divmod(g, NB)
                        slot = g % SLOTS
                        edges = packed[:, GK * q:GK * q + GK, bass.ds(blk * IB, IB)].bitcast(I32)
                        c_out = mask_c[:, slot, :, :].bitcast(I32)
                        compared.wait(compares)
                        signed.wait(signs)
                        masked.wait(groups_done)
                        word = BITS[bit] * 0x01010101
                        dve.scalar_tensor_tensor(c_out, sgn[:, g % SIGN_SLOTS, :, :].bitcast(I32), word, edges,
                                                 ALU.bitwise_and, ALU.bitwise_and).then_inc(c_ready, 1)
                        piece_of_half(0)
                        if g + 1 < NG:
                            compare(g + 1)
                        piece_of_half(1)
                        cut_c.wait(c_ready)
                        dve.scalar_tensor_tensor(mask_b[:, slot, :, :].bitcast(I32), edges, word, c_out,
                                                 ALU.bitwise_and, ALU.bitwise_xor).then_inc(b_ready, 1)
                        piece_of_half(2)
                        if FIRST_PIECE <= g < FIRST_PIECE + len(PIECES):
                            piece = PIECES[g - FIRST_PIECE]
                            if a == 0:
                                with after_first(dve, half):
                                    piece(n, 1, 16 * half)
                            else:
                                piece(n, 0, 16 * half + 16)

                if near:
                    halves = (Count(dve, "packed_halves", 1),
                              [Count(dve, f"piece_loads{j}", 16, 16) for j in range(NPC)])
                    with dve.Fori(0, first_two) as two:
                        for a in range(2):
                            step(0, 2 * two + a, two, a, halves)
                    for two in range(first_two, NIB // 2):
                        for a in range(2):
                            step(0, 2 * two + a, two, a, halves if two == first_two and a == 0 else None)
                with dve.Fori(1 if near else 0, H) as head:
                    with dve.Fori(0, NIB // 2) as two:
                        for a in range(2):
                            step(head, 2 * two + a, head * (NIB // 2) + two, a)
                for piece in PIECES:
                    piece(STEPS, 1, 16 * (STEPS // 2))

            return sync_program, gpsimd_program, tensor_program, scalar_program, vector_program

        wide, near = attention(WIDE), attention(NEAR)

        def load_flag(eng):
            return eng.value_load(flag[0:1, 0:1], min_val=0, max_val=1)

        with nc.Block() as block:
            @block.sync
            def _(sp):
                with sp.If(load_flag(sp) > 0):
                    with sp.Fori(0, NH2 // 2) as m:
                        for half in range(2):
                            for j in range(NPC):
                                sp.wait_ge(piece_ready, NPC * (2 * m + half) + j + 1)
                                load_piece(sp, NT1 + m, half, j)

            @block.gpsimd
            def _(pool):
                for s, k in ((piece_ready, NPC), (half_packed, 2), (half_copied, COPIES0)):
                    pool.nop().then_inc(s, k)

            @block.vector
            def _(dve):
                with dve.If(load_flag(dve) > 0):
                    counts = (Count(dve, "wide_packed", 1),
                              [Count(dve, f"wide_loads{j}", 16, 16) for j in range(NPC)])
                    with dve.Fori(0, NH2 // 2):
                        for half in range(2):
                            compare_half(dve, half, *counts)

            @block.tensor
            def _(pe):
                with pe.If(load_flag(pe) > 0):
                    counts = Count(pe, "wide_pieces", 2 * NPC, NPC), Count(pe, "wide_copies", COPIES0)
                    with pe.Fori(0, NH2 // 2):
                        for half in range(2):
                            pack_half(pe, half, *counts)

            @block.scalar
            def _(act):
                with act.If(load_flag(act) > 0):
                    count = Count(act, "wide_halves", 3)
                    with act.Fori(0, NH2 // 2) as m:
                        for half in range(2):
                            copy_half(act, NT1 + m, half, count)

        with nc.Block() as block:
            def chosen(eng, which):
                is_wide = load_flag(eng)
                with eng.If(is_wide > 0):
                    wide[which](eng)
                with eng.If(is_wide < 1):
                    near[which](eng)

            @block.sync
            def _(sp):
                chosen(sp, 0)

            @block.gpsimd
            def _(pool):
                chosen(pool, 1)

            @block.tensor
            def _(pe):
                chosen(pe, 2)

            @block.scalar
            def _(act):
                chosen(act, 3)

            @block.vector
            def _(dve):
                chosen(dve, 4)


_INS = ("x", "adj", "L0_gnn_W", "L0_gnn_b", "L0_gnn_aw")


def kernel(**inputs):
    import numpy as np
    import concourse.bacc as bacc
    from concourse.bass_utils import run_bass_kernel_spmd

    nc = bacc.Bacc("TRN2", target_bir_lowering=False, num_devices=1)
    arrays, args = {}, []
    for name in _INS:
        a = np.ascontiguousarray(inputs[name])
        arrays[f"in_{name}"] = a
        args.append(nc.dram_tensor(f"in_{name}", a.shape, mybir.dt.from_np(a.dtype), kind="ExternalInput").ap())
    h_dram = nc.dram_tensor("h_scratch", (N, F), F32).ap()
    s_dram = nc.dram_tensor("s_scratch", (H, N), F32).ap()
    out = nc.dram_tensor("out", (N, F), F32, kind="ExternalOutput").ap()
    gat_kernel(nc, *args, h_dram, s_dram, out)
    r = run_bass_kernel_spmd(nc, [arrays], core_ids=[0])
    return r.results[0]["out"]
```
